# Optimizing a Trainium2 kernel written in Bass

```python
import numpy as np
import jax
import jax.numpy as jnp

def _softmax(x, axis=-1):
    return jax.nn.softmax(x, axis=axis)

def _gelu(x):
    return jax.nn.gelu(x, approximate=True)

def _silu(x):
    return jax.nn.silu(x)

def _sigmoid(x):
    return jax.nn.sigmoid(x)

def _layernorm(x, axis=-1, eps=1e-05):
    m = jnp.mean(x, axis=axis, keepdims=True)
    v = jnp.var(x, axis=axis, keepdims=True)
    return (x - m) / jnp.sqrt(v + eps)

def _scatter_add(tgt, idx, src, axis=0):
    return tgt.at[idx].add(src)

def _segment_sum(src, seg, n):
    return jax.ops.segment_sum(src, seg, n)
kernel_name = 'mk_adaln_d1_jaxref_r8_3ce4e8'

def setup_inputs(seed: int=0):
    np.random.seed(seed)
    _w = jnp.asarray

    def _L0_attn_setup():
        import jax, jax.numpy as jnp
        import numpy as np
        B, S, D = (4, 256, 128)
        H = 16
        HD = D // H
        key = jax.random.key(seed)
        ks = jax.random.split(key, 5)
        x = jax.random.normal(ks[0], (B, S, D), dtype=jnp.float32)
        w_qkv = jax.random.normal(ks[1], (3 * D, D), dtype=jnp.float32) * (1.0 / np.sqrt(D))
        b_qkv = jax.random.normal(ks[2], (3 * D,), dtype=jnp.float32) * 0.01
        w_out = jax.random.normal(ks[3], (D, D), dtype=jnp.float32) * (1.0 / np.sqrt(D))
        b_out = jax.random.normal(ks[4], (D,), dtype=jnp.float32) * 0.01
        return {'x': x, 'w_qkv': w_qkv, 'b_qkv': b_qkv, 'w_out': w_out, 'b_out': b_out}
    _L0_attn_in = _L0_attn_setup()

    def _L0_ffn_setup():
        import jax, jax.numpy as jnp
        import numpy as np
        import math
        DMODEL = 128
        DFF = 512
        NUM_EXPERTS = 8
        TOPK = 2
        CAP_FACTOR = 1.25
        EPS = 1.1920929e-07

        def _trunc_normal(key, shape, fan_in, scale=1.0):
            std = scale * (1.0 / fan_in) ** 0.5
            return jax.random.truncated_normal(key, -2.0, 2.0, shape, jnp.float32) * std
        key = jax.random.key(seed)
        ks = jax.random.split(key, 5)
        return {'x': jax.random.normal(ks[0], (2, 256, DMODEL), jnp.float32), 'router_weight': _trunc_normal(ks[1], (NUM_EXPERTS, DMODEL), DMODEL), 'ff_pre_act_weight': _trunc_normal(ks[2], (NUM_EXPERTS, DFF, DMODEL), DMODEL), 'gate_weight': _trunc_normal(ks[3], (NUM_EXPERTS, DFF, DMODEL), DMODEL), 'ff_post_act_weight': _trunc_normal(ks[4], (NUM_EXPERTS, DMODEL, DFF), DFF)}
    _L0_ffn_in = _L0_ffn_setup()
    _L0_c = _w((lambda *s: np.random.randn(*s).astype(np.float32) * 0.05)(4, 128))
    _L0_wmod = _w((lambda *s: np.random.randn(*s).astype(np.float32) * 0.05)(128, 6 * 128) * 128 ** (-0.5))
    _d = {'L0_attn_x': _L0_attn_in['x'], 'L0_attn_w_qkv': _L0_attn_in['w_qkv'], 'L0_attn_b_qkv': _L0_attn_in['b_qkv'], 'L0_attn_w_out': _L0_attn_in['w_out'], 'L0_attn_b_out': _L0_attn_in['b_out'], 'L0_ffn_router_weight': _L0_ffn_in['router_weight'], 'L0_ffn_ff_pre_act_weight': _L0_ffn_in['ff_pre_act_weight'], 'L0_ffn_gate_weight': _L0_ffn_in['gate_weight'], 'L0_ffn_ff_post_act_weight': _L0_ffn_in['ff_post_act_weight'], 'L0_c': _L0_c, 'L0_wmod': _L0_wmod}
    _x0 = _d['L0_attn_x']
    _d['L0_attn_x'] = jax.random.normal(jax.random.fold_in(jax.random.key(seed), 1), (4, 1024, 128), dtype=_x0.dtype)
    del _x0
    return _d

def reference(L0_attn_x, L0_attn_w_qkv, L0_attn_b_qkv, L0_attn_w_out, L0_attn_b_out, L0_ffn_router_weight, L0_ffn_ff_pre_act_weight, L0_ffn_gate_weight, L0_ffn_ff_post_act_weight, L0_c, L0_wmod):

    def _L0_attn_ref(x, w_qkv, b_qkv, w_out, b_out):
        import jax, jax.numpy as jnp
        import numpy as np
        B, S, D = (4, 256, 128)
        H = 16
        HD = D // H
        b, s, d = x.shape
        qkv = x @ w_qkv.T + b_qkv
        q, k, v = jnp.split(qkv, 3, axis=2)
        q = q.reshape(b, s, H, HD).transpose(0, 2, 1, 3)
        k = k.reshape(b, s, H, HD).transpose(0, 2, 1, 3)
        v = v.reshape(b, s, H, HD).transpose(0, 2, 1, 3)
        att = jnp.einsum('bhqd,bhkd->bhqk', q, k) / np.sqrt(HD)
        causal = jnp.tril(jnp.ones((s, s), dtype=bool))
        att = jnp.where(causal[None, None], att, -jnp.inf)
        att = jax.nn.softmax(att, axis=-1)
        y = jnp.einsum('bhqk,bhkd->bhqd', att, v)
        y = y.transpose(0, 2, 1, 3).reshape(b, s, d)
        return y @ w_out.T + b_out

    def _L0_ffn_ref(x, router_weight, ff_pre_act_weight, gate_weight, ff_post_act_weight):
        import jax, jax.numpy as jnp
        import numpy as np
        import math
        DMODEL = 128
        DFF = 512
        NUM_EXPERTS = 8
        TOPK = 2
        CAP_FACTOR = 1.25
        EPS = 1.1920929e-07

        def _trunc_normal(key, shape, fan_in, scale=1.0):
            std = scale * (1.0 / fan_in) ** 0.5
            return jax.random.truncated_normal(key, -2.0, 2.0, shape, jnp.float32) * std
        orig_shape = x.shape
        h = x.reshape(-1, DMODEL)
        T = h.shape[0]
        logits = jnp.einsum('th,eh->te', h, router_weight)
        probs = jax.nn.softmax(logits.astype(jnp.float32), axis=-1)
        topk_probs, selected = jax.lax.top_k(probs, TOPK)
        topk_probs = topk_probs / jnp.maximum(topk_probs.sum(-1, keepdims=True), EPS)
        flat_tokens = jnp.repeat(jnp.arange(T), TOPK)
        flat_experts = selected.reshape(-1)
        flat_weights = topk_probs.reshape(-1)
        A = T * TOPK
        capacity = max(1, math.ceil(CAP_FACTOR * A / NUM_EXPERTS))
        weight_order = jnp.argsort(-flat_weights, stable=True)
        grouped_order = jnp.argsort(flat_experts[weight_order], stable=True)
        sort_order = weight_order[grouped_order]
        se = flat_experts[sort_order]
        st = flat_tokens[sort_order]
        sw = flat_weights[sort_order]
        counts = jnp.bincount(se, length=NUM_EXPERTS)
        offsets = jnp.cumsum(counts) - counts
        slot = jnp.arange(A) - offsets[se]
        keep = slot < capacity
        sw = jnp.where(keep, sw, 0.0)
        token_wsum = jnp.zeros(T, jnp.float32).at[st].add(sw)
        kept_w = sw / jnp.maximum(token_wsum[st], EPS)
        FC = NUM_EXPERTS * capacity
        dispatch = jnp.where(keep, se * capacity + slot, FC)
        expert_inputs = jnp.zeros((FC + 1, DMODEL), x.dtype).at[dispatch].set(h[st])
        expert_inputs = expert_inputs[:FC].reshape(NUM_EXPERTS, capacity, DMODEL)
        pre = jnp.einsum('ech,edh->ecd', expert_inputs, ff_pre_act_weight)
        gate = jnp.einsum('ech,edh->ecd', expert_inputs, gate_weight)
        expert_out = jnp.einsum('ecd,ehd->ech', pre * jax.nn.silu(gate), ff_post_act_weight)
        eo_flat = jnp.concatenate([expert_out.reshape(FC, DMODEL), jnp.zeros((1, DMODEL), x.dtype)], axis=0)
        updates = eo_flat[dispatch] * kept_w.astype(x.dtype)[:, None]
        out = jnp.zeros((T, DMODEL), x.dtype).at[st].add(updates)
        return out.reshape(orig_shape)
    x = L0_attn_x
    mod = (_silu(L0_c) @ L0_wmod).reshape(L0_c.shape[0], 6, 1, -1)
    sa, ca, ga, sb, cb, gb = (mod[:, 0], mod[:, 1], mod[:, 2], mod[:, 3], mod[:, 4], mod[:, 5])
    ga = (2 * (ga >= 0) - 1) * jnp.maximum(jnp.abs(ga), 0.25)
    gb = (2 * (gb >= 0) - 1) * jnp.maximum(jnp.abs(gb), 0.25)
    h = _layernorm(x, axis=-1) * (1 + ca) + sa
    x = x + ga * _L0_attn_ref(h, L0_attn_w_qkv, L0_attn_b_qkv, L0_attn_w_out, L0_attn_b_out)
    h = _layernorm(x, axis=-1) * (1 + cb) + sb
    x = x + gb * _L0_ffn_ref(h, L0_ffn_router_weight, L0_ffn_ff_pre_act_weight, L0_ffn_gate_weight, L0_ffn_ff_post_act_weight)
    return x

_drawn_inputs = setup_inputs


def setup_inputs(seed=0):
    import zlib

    import numpy as np

    out = dict(_drawn_inputs(seed))
    spreads = {}
    factors = {'L0_attn_b_qkv': 8.0, 'L0_attn_b_out': 8.0}
    for name, (base, spread) in spreads.items():
        noise = np.random.default_rng([zlib.crc32(name.encode()), seed]).standard_normal(out[name].shape)
        drawn = base * np.exp(spread * noise) if base else spread * noise
        out[name] = jnp.asarray(drawn.astype(out[name].dtype))
    for name, factor in factors.items():
        out[name] = (out[name] * factor).astype(out[name].dtype)
    return out
```

```python
from contextlib import ExitStack

import concourse.bass as bass
from concourse import mybir

ALU = mybir.AluOpType
ACT = mybir.ActivationFunctionType
F32 = mybir.dt.float32
BF16 = mybir.dt.bfloat16
I32 = mybir.dt.int32
AX = mybir.AxisListType

P = 128
NB, S, D = 4, 1024, 128
H, HD = 16, 8
GH = 4
NG = H // GH
NN = NB * NG
T = NB * S
NT = T // P
BT = S // P
NE, F = 8, 512
CAP = 1280
SLOTS = NE * CAP
ST = CAP // P
FC = F // P
ROW = D + 1
EPS_LN = 1e-5
EPS = 1.1920929e-07
NEG = -1e30
FAR = 1048576.0
SCALE = float(HD) ** -0.5

QUNITS = [
    [(4, 0, 512, 0, 0)],
    [(5, 0, 512, 0, 0)],
    [(6, 0, 512, 0, 0)],
    [(7, 0, 512, 0, 0)],
    [(3, 0, 512, 0, 0)],
    [(7, 512, 512, 0, 1)],
    [(0, 0, 128, 0, 0), (6, 512, 384, 128, 1)],
    [(4, 512, 128, 0, 1), (2, 0, 384, 128, 0)],
    [(1, 0, 256, 0, 0), (5, 512, 256, 256, 1)],
]
NQU = 2 * len(QUNITS)
KUNITS = [
    [(0, 0, 0, 512, 0)],
    [(1, 0, 128, 384, 0), (3, 0, 384, 128, 384)],
    [(2, 0, 256, 256, 0), (6, 1, 256, 256, 256)],
    [(0, 1, 0, 512, 0)],
    [(1, 1, 0, 512, 0)],
    [(2, 1, 0, 512, 0)],
    [(3, 1, 0, 512, 0)],
    [(4, 1, 0, 512, 0)],
    [(5, 1, 128, 384, 0), (7, 1, 384, 128, 384)],
]
NK = len(KUNITS)
NKU = GH * NK
NP = 3


def diagonal(piece):
    kb, qc, q0, w, col = piece
    return kb * P == qc * 512 + q0


MASKED = [any(diagonal(p) for p in kind) for kind in KUNITS]
NMASK = sum(MASKED)
QSTEP = [-1, -1] + [1 + u * 25 // (NQU - 2) for u in range(NQU - 2)]
MSTEP = 31


def after(engine, semaphore, count):
    if not (isinstance(count, int) and count <= 0):
        engine.wait_ge(semaphore, count)


def build(nc, x, wqkvT, bqkv, bv, woT, bout, rT, w1T, wgT, w2T, cT, wmod, out):
    with ExitStack() as ctx:
        def sb(name, shape, dt=F32):
            return ctx.enter_context(nc.sbuf_tensor(name, shape, dt))

        def sem(name):
            return ctx.enter_context(nc.semaphore(name))

        def dram(name, shape, dt=F32):
            return nc.dram_tensor(name, shape, dt, kind="Internal").ap()

        k_parts = dram("k_parts", [NN, 3, 32, S], BF16)
        q_parts = dram("q_parts", [NN, 3, 32, S], BF16)
        slot_rows = dram("slot_rows", [SLOTS, ROW])
        results = dram("results", [2 * T, D])

        xs = sb("xs", [P, NT, D])
        vals = sb("vals", [P, NN, BT, 32])
        ys = sb("ys", [P, NN, BT, 32])
        modrow = sb("modrow", [P, NB, 4, D])
        rT_s = sb("rT_s", [P, NE])
        wo_s = sb("wo_s", [P, D])
        bo_row = sb("bo_row", [P, D])
        identf = sb("identf", [P, P])
        identb = sb("identb", [P, P], BF16)
        cmask = sb("cmask", [P, P], BF16)
        before = sb("before", [P, P], BF16)
        onesb = sb("onesb", [P, P], BF16)
        stats = sb("stats", [P, BT, 6])
        mv = sb("mv", [P, BT, 2])
        vpe = sb("vpe", [P, BT])
        rstd = sb("rstd", [P, BT])
        mhalf = sb("mhalf", [P, BT])
        fill = sb("fill", [P, ROW])

        stack = sb("stack", [P, 2 * NG * GH * S // 2])
        stacks = [stack[:, i * 2 * S:(i + 1) * 2 * S].bitcast(BF16).rearrange("p (h q) -> p h q", h=GH)
                  for i in range(2 * NG)]
        qst, kst = stacks[:NG], stacks[NG:]
        vst = [sb(f"vst{i}", [P, BT, GH, 32]) for i in range(2)]
        prob_all = sb("prob_all", [P, NP * GH * 512])
        probs = [prob_all[:, i * 2048:(i + 1) * 2048].rearrange("p (h q) -> p h q", h=GH) for i in range(NP)]
        osb = [sb(f"osb{i}", [P, 512]) for i in range(2)]
        mx = sb("mx", [P, 2, GH, BT])
        mparts = sb("mparts", [P, 3, GH, BT], BF16)
        mres = sb("mres", [P, GH, BT])
        mT = sb("mT", [96, P], BF16)
        rec = sb("rec", [P, BT // 2, GH])

        wqkv_s = sb("wqkv_s", [P, 3 * D])
        bqkv_s = sb("bqkv_s", [P, 3])
        bv_row = sb("bv_row", [P, D])
        ct = sb("ct", [P, NB])
        et = sb("et", [P, NB])
        sc = sb("sc", [P, NB])
        wmod_s = prob_all[:, 0:6 * D]
        scb = prob_all[:, 768:768 + NB * P].rearrange("p (b q) -> p b q", b=NB)
        gneg = prob_all[:, 1280:1280 + 2 * NB * D].rearrange("p (b a d) -> p b a d", b=NB, a=2)
        gsgn = prob_all[:, 2304:2304 + 2 * NB * D].rearrange("p (b a d) -> p b a d", b=NB, a=2)
        modcol = sb("modcol", [P, 2, NB])
        xn = [sb(f"xn{i}", [P, 4, D]) for i in range(2)]
        hT = [sb(f"hT{i}", [P, 512]) for i in range(2)]
        early = sb("early", [P, 12 * 256 + 2 * BT * ROW])
        parts = [[early[:, (2 * i + j) * 768:(2 * i + j) * 768 + 768].bitcast(BF16)
                  .rearrange("p (a q) -> p a q", a=3) for j in range(2)] for i in range(2)]
        pres = [[early[:, 3072 + (2 * i + j) * 512:3584 + (2 * i + j) * 512] for j in range(2)] for i in range(2)]

        wog = sb("wog", [P, NB, D])
        gab = sb("gab", [P, NB, D])
        stats2 = [sb(f"stats2{i}", [P, 4, 6]) for i in range(2)]
        mv2 = [sb(f"mv2{i}", [P, 4, 2]) for i in range(2)]
        vpe2 = [sb(f"vpe2{i}", [P, 4]) for i in range(2)]
        rstd2 = [sb(f"rstd2{i}", [P, 4]) for i in range(2)]
        yc, yT = xn, hT
        h2T = [xn[i][:].rearrange("p t d -> p (t d)") for i in range(2)]
        rows = early[:, 3072:3072 + 2 * BT * ROW].rearrange("p (k t r) -> p k t r", k=2, t=BT)
        dests = sb("dests", [P, 2, NT], I32)
        lg, pr, eqb, tvb = (sb(f"{n}", [P, BT, NE]) for n in ("lg", "pr", "eqb", "tvb"))
        topb = sb("topb", [P, 4, BT])
        m1b, smb, first1b, first2b = (topb[:, i, :] for i in range(4))
        maskbb = sb("maskbb", [P, NE, BT], BF16)
        scanb, exclb, rankb, overb = (sb(f"{n}", [P, NE, BT]) for n in ("scanb", "exclb", "rankb", "overb"))
        used = sb("used", [P, NE])
        shift = sb("shift", [P, NE])
        idxb = sb("idxb", [P, 2, BT], I32)
        oh1, oh2 = sb("oh1", [P, NT, NE]), sb("oh2", [P, NT, NE])

        tile_no = iter(range(24))

        def rt(by_expert=False):
            i = next(tile_no)
            v = prob_all[:, i * 256:(i + 1) * 256]
            return v.rearrange("p (e t) -> p e t", e=NE) if by_expert else v.rearrange("p (t e) -> p t e", e=NE)

        eq, wa, wb = (rt() for _ in range(3))
        wsel, cmp_, keep, rank, slot, scan1, excl = (rt(True) for _ in range(7))
        prod = rt()
        small = sb("small", [P, 11, NT])
        sm, pm1, pm2, w1s, w2s, keep1, keep2, kw1, kw2, slot1, slot2 = (small[:, i, :] for i in range(11))
        kept_rows = vals[:].rearrange("p n t d -> p (n t d)").rearrange("p (t d) -> p t d", d=D)
        idx = sb("idx", [P, 2, NT], I32)
        rev_i = sb("rev_i", [P, 2, NE], I32)
        rev = sb("rev", [P, 2, NE])
        thr = sb("thr", [P, NE], I32)
        cand = sb("cand", [P, NE], I32)
        bit = sb("bit", [P, NE], I32)
        acc = sb("acc", [P, NE])
        need = sb("need", [P, NE])
        redo = sb("redo", [P, 1], I32)
        onesf = sb("onesf", [P, NE * NT])
        part8 = sb("part8", [P, NE], BF16)
        maskb = sb("maskb", [P, NE, NT], BF16)

        w1_s = [early[:, i * F:i * F + F] for i in range(2)]
        wg_s = [early[:, (2 + i) * F:(3 + i) * F] for i in range(2)]
        w2_s = [early[:, (4 + i) * F:(5 + i) * F].rearrange("p (c d) -> p c d", c=FC) for i in range(2)]

        def cut(o, n):
            return stack[:, o:o + n]

        NX = ST * ROW
        xr = [cut(i * NX, NX).rearrange("p (s r) -> p s r", s=ST) for i in range(2)]
        xT = [cut(2 * NX + i * CAP, CAP) for i in range(2)]
        hid = [cut(2 * NX + 2 * CAP + i * FC * 512, FC * 512).rearrange("p (f n) -> p f n", f=FC) for i in range(2)]
        sg = [hT[i] for i in range(2)]
        yo = [prob_all[:, i * CAP:(i + 1) * CAP].rearrange("p (s d) -> p s d", s=ST) for i in range(2)]

        g1 = vals[:].rearrange("p n t d -> p (n t d)").rearrange("p (t d) -> p t d", d=D)
        g2 = ys[:].rearrange("p n t d -> p (n t d)").rearrange("p (t d) -> p t d", d=D)

        psum = ctx.enter_context(nc.psum_tensor("psum", [P, 8, 512], F32))

        x_in = [sem(f"x_in{q}") for q in range(4)]
        w_in, wmod_in = sem("w_in"), sem("wmod_in")
        consts_ready, fill_ready, filled = sem("consts_ready"), sem("fill_ready"), sem("filled")
        exp_c, one_c, rec_c, silu_c, wide_c = (sem(n) for n in ("exp_c", "one_c", "rec_c", "silu_c", "wide_c"))
        modcol_mm, modcol_ready, modrow_mm, modrow_copied = (
            sem(n) for n in ("modcol_mm", "modcol_ready", "modrow_mm", "modrow_copied"))
        gates_ready = sem("gates_ready")
        ln_stats, ln_aggr, ln_eps, ln_rstd, ln_norm = (
            sem(n) for n in ("ln_stats", "ln_aggr", "ln_eps", "ln_rstd", "ln_norm"))
        xT_mm, hT_ready, qk_mm, v_mm = (sem(n) for n in ("xT_mm", "hT_ready", "qk_mm", "v_mm"))
        part_hi, part_res, part_mid, part_lo, v_ready = (
            sem(n) for n in ("part_hi", "part_res", "part_mid", "part_lo", "v_ready"))
        parts_out = [sem(f"parts_out{i}") for i in range(2)]
        stacks_clear, v_staged = sem("stacks_clear"), sem("v_staged")
        staged = [sem(f"staged{i}") for i in range(NG)]
        q_scores, maxed, k_scores, exped, masked = (
            sem(n) for n in ("q_scores", "maxed", "k_scores", "exped", "masked"))
        pv_done, o_copied, oT_mm, o_rec, o_norm = (
            sem(n) for n in ("pv_done", "o_copied", "oT_mm", "o_rec", "o_norm"))
        m_step, mT_mm, mT_copied, m_rows = (sem(n) for n in ("m_step", "mT_mm", "mT_copied", "m_rows"))
        pool_waited, act_waited, dve_waited = sem("pool_waited"), sem("act_waited"), sem("dve_waited")
        gates_folded, y_cont, yT_mm, yT_ready, proj_mm, bias_in, x1_ready = (
            sem(n) for n in ("gates_folded", "y_cont", "yT_mm", "yT_ready", "proj_mm", "bias_in", "x1_ready"))
        n2_stats, n2_aggr, n2_step, rstd2_ready, h2_step, h2_ready, h2_kept, h2T_mm, h2T_ready = (
            sem(n) for n in ("n2_stats", "n2_aggr", "n2_step", "rstd2_ready", "h2_step", "h2_ready", "h2_kept",
                             "h2T_mm", "h2T_ready"))
        logit_mm, logit_ready, route_step, lg_shifted, exp_l, chosen, prefix_mm, prefix_read, idx_ready, scattered = (
            sem(n) for n in ("logit_mm", "logit_ready", "route_step", "lg_shifted", "exp_l", "chosen", "prefix_mm",
                             "prefix_read", "idx_ready", "scattered"))
        iotas, rev_ready, dest_ready, dest_in = (sem(n) for n in ("iotas", "rev_ready", "dest_ready", "dest_in"))
        redo_ready, last_step, redo_step, chosen_part, chosen_mm, above_part, above_mm = (
            sem(n) for n in ("redo_ready", "last_step", "redo_step", "chosen_part", "chosen_mm", "above_part",
                             "above_mm"))
        bis_step, bis_part, bis_count, redo_prefix_in, redo_prefix_mm, redo_idx, redo_rows, resent, dispatched = (
            sem(n) for n in ("bis_step", "bis_part", "bis_count", "redo_prefix_in", "redo_prefix_mm", "redo_idx",
                             "redo_rows", "resent", "dispatched"))
        rows_in = [sem(f"rows_in{i}") for i in range(2)]
        weights_in = [sem(f"weights_in{i}") for i in range(2)]
        rT_mm, rT_ready, up_mm, silu_ready, hid_ready, down_mm, y_ready = (
            sem(n) for n in ("rT_mm", "rT_ready", "up_mm", "silu_ready", "hid_ready", "down_mm", "y_ready"))
        sent = [sem(f"sent{i}") for i in range(2)]
        res_in = [sem(f"res_in{b}") for b in range(NB)]
        scaled, summed, gated, finished = (sem(n) for n in ("scaled", "summed", "gated", "finished"))
        ended = sem("ended")

        block = ctx.enter_context(nc.Block())

        QB = [0, 2]
        KB = [4, 5]
        PV, MISC = 6, 7

        def masks_before(kind):
            return sum(MASKED[:kind])

        @block.sync
        def _(sp):
            sp.dma_start(ct[:], cT).then_inc(wmod_in, 16)
            sp.dma_start(wmod_s[:], wmod).then_inc(wmod_in, 16)
            for c in range(4):
                sp.dma_start(xs[:, 8 * c:8 * c + 8, :],
                             x.rearrange("b (t p) d -> p (b t) d", p=P)[:, 8 * c:8 * c + 8, :]).then_inc(x_in[c], 16)
            sp.dma_start(wqkv_s[:], wqkvT).then_inc(w_in, 16)
            sp.dma_start(bqkv_s[:], bqkv).then_inc(w_in, 16)
            sp.dma_start(bv_row[:], bv.to_broadcast([P, D])).then_inc(w_in, 16)
            sp.dma_start(bo_row[:], bout.to_broadcast([P, D])).then_inc(w_in, 16)
            sp.dma_start(wo_s[:], woT).then_inc(w_in, 16)
            sp.dma_start(rT_s[:], rT).then_inc(w_in, 16)

            sp.wait_ge(fill_ready, 3)
            sp.dma_start(slot_rows.rearrange("(p s) r -> p s r", p=P),
                         fill[:].unsqueeze(1).to_broadcast([P, SLOTS // P, ROW])).then_inc(filled, 16)
            sp.dma_start(results.rearrange("(p s) r -> p s r", p=P),
                         fill[:, 0:D].unsqueeze(1).to_broadcast([P, 2 * T // P, D])).then_inc(filled, 16)
            def parts_to_dram(b):
                for half in range(2):
                    for j, dst in enumerate((q_parts, k_parts)):
                        sp.wait_ge(part_lo, b * 4 + 2 * half + j + 1)
                        for part in range(3):
                            sp.dma_start(dst[bass.ds(b * NG, NG), part, :, 512 * half:512 * half + 512],
                                         parts[half][j][:, part, :]).then_inc(parts_out[half], 16)

            def stage(n, buf):
                for src, dst, runs in (
                    (q_parts, qst[buf], ((0, 0, 1), (8, 0, 1), (16, 0, 1), (24, 1, 1), (32, 1, 1), (40, 2, 1))),
                    (k_parts, kst[buf], ((0, 0, 3), (24, 0, 2), (40, 0, 1))),
                ):
                    for row, part, k in runs:
                        sp.dma_start(dst[row:row + 8 * k, :, :].rearrange("p h q -> p (h q)"),
                                     src[bass.ds(n, 1), part:part + k, :, :]
                                     .rearrange("n k (d h) q -> (n k d) (h q)", h=GH)).then_inc(staged[buf], 16)

            def m_move(n, buf):
                sp.wait_ge(mT_copied, n + 1)
                for part in range(3):
                    sp.dma_start(qst[buf][96 + part:97 + part, :, :].rearrange("p h (i q) -> p (h i) q", q=P),
                                 mT[32 * part:32 * part + 32, :]).then_inc(m_rows, 16)

            parts_to_dram(0)
            for half in range(2):
                sp.wait_ge(parts_out[half], 96 + 1)
            sp.wait_ge(stacks_clear, 2 * NG)
            stage(0, 0)
            with sp.Fori(1, NB) as b:
                parts_to_dram(b)
            for n in range(1, NG):
                stage(n, n)
            for half in range(2):
                sp.wait_ge(parts_out[half], 96 * NB + 1)
            m_move(0, 0)

            def load_weights(e, q):
                sp.dma_start(w1_s[q][:], w1T[bass.ds(e, 1), :, :].rearrange("e h f -> (e h) f")
                             ).then_inc(weights_in[q], 16)
                sp.dma_start(wg_s[q][:], wgT[bass.ds(e, 1), :, :].rearrange("e h f -> (e h) f")
                             ).then_inc(weights_in[q], 16)
                sp.dma_start(w2_s[q][:], w2T[bass.ds(e, 1), :, :].rearrange("e (c p) h -> p (e c) h", p=P)
                             ).then_inc(weights_in[q], 16)

            def load_rows(e, q):
                sp.dma_start(xr[q], slot_rows[bass.ds(e * CAP, CAP), :].rearrange("(s p) r -> p s r", p=P)
                             ).then_inc(rows_in[q], 16)

            for q in range(2):
                load_weights(q, q)

            def group(b, m, more):
                n = b * NG + m
                m_move(n + 1, (m + 1) % NG)
                if more:
                    sp.wait_ge(k_scores, n * NKU + NKU)
                    stage(n + NG, m)

            with sp.Fori(0, NB - 1) as b:
                for m in range(NG):
                    group(b, m, True)
            for m in range(NG - 1):
                group(NB - 1, m, False)
            sp.wait_ge(k_scores, NN * NKU)
            sp.wait_ge(dispatched, 1)
            for q in range(2):
                load_rows(q, q)
            with sp.Fori(0, 3) as j:
                for q in range(2):
                    sp.wait_ge(down_mm, (j * 2 + q) * 3 + 3)
                    load_weights(j * 2 + q + 2, q)
                    sp.wait_ge(sent[q], j * (16 * ST) + 16 * ST)
                    load_rows(j * 2 + q + 2, q)
            for q in range(2):
                sp.wait_ge(sent[q], 4 * 16 * ST)
            for b in range(NB):
                for k, g in enumerate((g1, g2)):
                    sp.dma_start(g[:, b * BT:b * BT + BT, :],
                                 results[k * T + b * S:k * T + b * S + S, :].rearrange("(t p) d -> p t d", p=P)
                                 ).then_inc(res_in[b], 16)
            for b in range(NB):
                sp.wait_ge(finished, b + 1)
                sp.dma_start(out[b].rearrange("(t p) d -> p t d", p=P), g1[:, b * BT:b * BT + BT, :]
                             ).then_inc(ended, 16)
            sp.wait_ge(ended, 16 * NB)

        @block.gpsimd
        def _(pool):
            for one in parts_out:
                pool.sem_inc(one, 1)
            nc.gpsimd.memset(fill[:], 0.0).then_inc(fill_ready, 1)
            pool.wait_ge(fill_ready, 1)
            nc.gpsimd.memset(fill[:, D:ROW].bitcast(I32), int(FAR)).then_inc(fill_ready, 2)
            nc.gpsimd.memset(mhalf[:], -0.5).then_inc(consts_ready, 1)
            for m in (identf, identb):
                nc.gpsimd.memset(m[:], 0.0).then_inc(consts_ready, 1)
            nc.gpsimd.memset(cmask[:], 0.0).then_inc(consts_ready, 1)
            nc.gpsimd.memset(before[:], 1.0).then_inc(consts_ready, 1)
            nc.gpsimd.memset(onesb[:], 1.0).then_inc(consts_ready, 1)
            pool.wait_ge(consts_ready, 6)
            for m in (identf, identb):
                nc.gpsimd.affine_select(out=m[:], in_=m[:], compare_op=ALU.not_equal, fill=1.0, base=0,
                                        pattern=[[-1, P]], channel_multiplier=1).then_inc(consts_ready, 1)
            nc.gpsimd.affine_select(out=cmask[:], in_=cmask[:], compare_op=ALU.is_ge, fill=NEG, base=0,
                                    pattern=[[-1, P]], channel_multiplier=1).then_inc(consts_ready, 1)
            nc.gpsimd.affine_select(out=before[:], in_=before[:], compare_op=ALU.is_gt, fill=0.0, base=0,
                                    pattern=[[1, P]], channel_multiplier=-1).then_inc(consts_ready, 1)
            for i in range(2):
                nc.gpsimd.memset(stack[:, 2048 * (NG + i):2048 * (NG + i) + 2048], 0.0).then_inc(stacks_clear, 1)
            def deviation(b):
                pool.wait_ge(ln_eps, b + 1)
                nc.gpsimd.tensor_tensor(rstd[:], vpe[:], mhalf[:], ALU.pow).then_inc(ln_rstd, 1)

            deviation(0)
            for i in range(2, NG):
                nc.gpsimd.memset(stack[:, 2048 * (NG + i):2048 * (NG + i) + 2048], 0.0).then_inc(stacks_clear, 1)
            deviation(1)
            for i in range(2):
                nc.gpsimd.memset(vst[i][:], 0.0).then_inc(v_staged, 1)

            def low_parts(b):
                for half in range(2):
                    for j in range(2):
                        pool.wait_ge(part_mid, b * 4 + 2 * half + j + 1)
                        pool.sem_inc(pool_waited, 1)
                        nc.gpsimd.tensor_tensor(parts[half][j][:, 2, :], pres[half][j], parts[half][j][:, 1, :],
                                                ALU.subtract).then_inc(part_lo, 1)

            low_parts(0)
            with pool.Fori(1, NB - 1) as b:
                deviation(b + 1)
                low_parts(b)
            low_parts(NB - 1)
            pool.wait_ge(stacks_clear, 2 * NG)
            pool.wait_ge(v_staged, 2)
            pool.wait_ge(part_lo, 4 * NB)
            for i in range(NG):
                nc.gpsimd.memset(stack[96:99, 2048 * (NG + i):2048 * (NG + i) + 2048].bitcast(I32), 0x3F803F80
                                 ).then_inc(stacks_clear, 1)
                pool.wait_ge(stacks_clear, 2 * NG + 1 + i)
            for i in range(2):
                nc.gpsimd.memset(vst[i][:, :, :, HD:HD + 1], 1.0).then_inc(v_staged, 1)
            nc.gpsimd.iota(rev_i[:, 0, :], pattern=[[-1, NE]], base=NE, channel_multiplier=0).then_inc(iotas, 1)
            nc.gpsimd.iota(rev_i[:, 1, :], pattern=[[CAP, NE]], base=0, channel_multiplier=0).then_inc(iotas, 1)
            nc.gpsimd.memset(onesf[:], 1.0).then_inc(iotas, 1)
            nc.gpsimd.memset(used[:], 0.0).then_inc(iotas, 1)
            nc.gpsimd.memset(small[:], 1.0).then_inc(iotas, 1)
            nc.gpsimd.iota(dests[:], pattern=[[T, 2], [P, NT]], base=0, channel_multiplier=1).then_inc(dest_ready, 1)

            def stage_v(n, buf):
                nc.gpsimd.tensor_copy(
                    vst[buf][:, :, :, 0:HD],
                    vals[:, bass.ds(n, 1), :, :].rearrange("p n t (h d) -> p (n t) h d", h=GH)
                ).then_inc(v_staged, 1)

            pool.wait_ge(v_ready, 2 * NB)
            pool.wait_ge(v_staged, 4)
            stage_v(0, 0)
            pool.wait_ge(gates_ready, 6)
            pool.wait_ge(w_in, 96)
            for b in range(NB):
                nc.gpsimd.tensor_tensor(wog[:, b, :], wo_s[:], modrow[:, b, 0, :], ALU.mult).then_inc(gates_folded, 1)
                nc.gpsimd.tensor_tensor(gab[:, b, :], bo_row[:], modrow[:, b, 0, :], ALU.mult
                                        ).then_inc(gates_folded, 1)
            pool.wait_ge(gates_folded, 2 * NB)
            pool.wait_ge(dest_ready, 1)
            pool.wait_ge(filled, 32)

            def gather_heads(b):
                pool.wait_ge(o_norm, b * (2 * NG) + 2 * NG)
                pool.sem_inc(pool_waited, 1)
                for half in range(2):
                    nc.gpsimd.tensor_copy(
                        yc[half][:].rearrange("p t (g d) -> p t g d", g=NG),
                        ys[:, bass.ds(b * NG, NG), 4 * half:4 * half + 4, :].rearrange("p g t d -> p t g d")
                    ).then_inc(y_cont, 1)
                for half in range(2):
                    xv = xs[:, bass.ds(b * BT + 4 * half, 4), :]
                    nc.gpsimd.tensor_tensor(xv, xv, gab[:, bass.ds(b, 1), :].to_broadcast([P, 4, D]),
                                            ALU.add).then_inc(bias_in, 1)

            def second_norm(b, half):
                c = b * 2 + half
                pool.wait_ge(n2_step, c + 1)
                nc.gpsimd.tensor_tensor(rstd2[half][:], vpe2[half][:], mhalf[:, 0:4], ALU.pow
                                        ).then_inc(rstd2_ready, 1)
                h = rows[:, 0, 4 * half:4 * half + 4, 0:D]
                nc.gpsimd.tensor_tensor(h, xs[:, bass.ds(c * 4, 4), :],
                                        mv2[half][:, :, 0:1].to_broadcast([P, 4, D]), ALU.subtract
                                        ).then_inc(h2_step, 1)
                pool.wait_ge(rstd2_ready, c + 1)
                pool.wait_ge(h2_step, c * 3 + 1)
                nc.gpsimd.tensor_tensor(h, h, rstd2[half][:].unsqueeze(2).to_broadcast([P, 4, D]), ALU.mult
                                        ).then_inc(h2_step, 1)
                pool.wait_ge(h2_step, c * 3 + 2)
                pool.sem_inc(pool_waited, 1)
                nc.gpsimd.tensor_tensor(h, h, modrow[:, bass.ds(b, 1), 2, :].to_broadcast([P, 4, D]), ALU.mult
                                        ).then_inc(h2_step, 1)
                pool.wait_ge(h2_step, c * 3 + 3)
                pool.sem_inc(pool_waited, 1)
                nc.gpsimd.tensor_tensor(h, h, modrow[:, bass.ds(b, 1), 1, :].to_broadcast([P, 4, D]), ALU.add
                                        ).then_inc(h2_ready, 1)
                pool.wait_ge(h2_ready, c + 1)
                pool.sem_inc(pool_waited, 1)
                nc.gpsimd.tensor_copy(rows[:, 1, 4 * half:4 * half + 4, 0:D], h).then_inc(h2_kept, 1)
                nc.gpsimd.tensor_copy(kept_rows[:, bass.ds(c * 4, 4), :], h).then_inc(h2_kept, 1)
                if half == 0:
                    nc.gpsimd.tensor_copy(rows[:, :, :, D:ROW].bitcast(I32).rearrange("p k t r -> p k (t r)"),
                                          dests[:, :, bass.ds(b * BT, BT)]).then_inc(dest_in, 1)

            def scatter(b):
                pool.wait_ge(idx_ready, b * 2 + 2)
                pool.wait_ge(h2_kept, b * 4 + 4)
                pool.wait_ge(dest_in, b + 1)
                pool.sem_inc(pool_waited, 1)
                for t in range(BT):
                    for k in range(2):
                        nc.gpsimd.indirect_dma_start(
                            slot_rows, bass.IndirectOffsetOnAxis(ap=idxb[:, k, t:t + 1], axis=0),
                            rows[:, k, t, :], None, bounds_check=SLOTS - 1, oob_is_err=False).then_inc(scattered, 16)

            def group(b, m, last, mix):
                n = b * NG + m
                for kind in range(NK):
                    if MASKED[kind]:
                        pool.wait_ge(exped, n * NKU + GH * kind + GH)
                        pool.sem_inc(pool_waited, 1)
                        done = [p for p in KUNITS[kind] if diagonal(p)]
                        for piece in done:
                            col = piece[4]
                            v = probs[kind % NP][:, :, col:col + P]
                            ins = nc.gpsimd.affine_select(out=v, in_=v, compare_op=ALU.is_ge, fill=0.0, base=0,
                                                          pattern=[[0, GH], [1, P]], channel_multiplier=-1)
                        ins.then_inc(masked, 1)
                    if kind == 2:
                        if not last:
                            after(pool, pv_done, n * NK)
                            pool.sem_inc(pool_waited, 1)
                            stage_v(n + 1, (m + 1) % 2)
                        if mix and m == 0:
                            gather_heads(b - 1)
                        if mix and m == 1:
                            second_norm(b - 1, 0)
                            second_norm(b - 1, 1)
                        if mix and m == 3:
                            scatter(b - 1)
                if mix and m == 3:
                    pool.wait_ge(scattered, b * (32 * BT))

            for m in range(NG):
                group(0, m, False, False)
            with pool.Fori(1, NB - 1) as b:
                for m in range(NG):
                    group(b, m, False, True)
            for m in range(NG):
                group(NB - 1, m, m == NG - 1, True)
            gather_heads(NB - 1)
            second_norm(NB - 1, 0)
            second_norm(NB - 1, 1)
            scatter(NB - 1)
            pool.wait_ge(redo_ready, 1)
            again = pool.value_load(redo[0:1, 0:1], min_val=0, max_val=1)
            pool.wait_ge(scattered, NB * 32 * BT)
            with pool.If(again > 0):
                pool.wait_ge(redo_idx, 2)
                for b in range(NB):
                    for k in range(2):
                        nc.gpsimd.tensor_copy(rows[:, k, :, 0:D], kept_rows[:, b * BT:b * BT + BT, :]
                                              ).then_inc(redo_rows, 1)
                    nc.gpsimd.tensor_copy(rows[:, :, :, D:ROW].bitcast(I32).rearrange("p k t r -> p k (t r)"),
                                          dests[:, :, b * BT:b * BT + BT]).then_inc(redo_rows, 1)
                    pool.wait_ge(redo_rows, 3 * b + 3)
                    for t in range(BT):
                        for k in range(2):
                            nc.gpsimd.indirect_dma_start(
                                slot_rows, bass.IndirectOffsetOnAxis(ap=idx[:, k, b * BT + t:b * BT + t + 1], axis=0),
                                rows[:, k, t, :], None, bounds_check=SLOTS - 1, oob_is_err=False
                            ).then_inc(resent, 16)
                    pool.wait_ge(resent, (b + 1) * 32 * BT)
            pool.sem_inc(dispatched, 1)

            def send(e, q, col=0):
                pool.wait_ge(y_ready, e * 3 + 3)
                pool.sem_inc(pool_waited, 1)
                for st in range(ST):
                    nc.gpsimd.indirect_dma_start(
                        results, bass.IndirectOffsetOnAxis(ap=xr[q][:, st, D:ROW].bitcast(I32), axis=0),
                        yo[q][:, st, :], None, bounds_check=2 * T - 1, oob_is_err=False).then_inc(sent[q], 16)

            with pool.Fori(0, NE // 2) as j:
                for q in range(2):
                    send(j * 2 + q, q)

        @block.tensor
        def _(pe):
            pe.wait_ge(wmod_in, 32)
            pe.wait_ge(silu_c, 1)
            for j in range(2):
                mm = nc.tensor.matmul(psum[:, MISC, j * NB:j * NB + NB], wmod_s[:, j * D:j * D + D], sc[:],
                                      start=True, stop=True)
            mm.then_inc(modcol_mm, 1)
            pe.wait_ge(wide_c, 1)
            for b in range(NB):
                nc.tensor.matmul(psum[:, b, :], scb[:, b, :], wmod_s[:, 2 * D:6 * D],
                                 start=True, stop=True).then_inc(modrow_mm, 1)
            pe.wait_ge(consts_ready, 10)
            pe.wait_ge(w_in, 96)
            pe.wait_ge(modrow_copied, 2 * NB)

            def turn_normed(b, half):
                pe.wait_ge(ln_norm, b * 2 + half + 1)
                for i in range(4):
                    mm = nc.tensor.transpose(psum[:, half, i * P:i * P + P], xn[half][:, i, :], identf[:])
                mm.then_inc(xT_mm, 1)

            def project(b, half):
                pe.wait_ge(hT_ready, b * 2 + half + 1)
                for j in range(2):
                    nc.tensor.matmul(psum[:, 2 + 2 * j + half, :], wqkv_s[:, j * D:j * D + D], hT[half][:],
                                     start=True, stop=True).then_inc(qk_mm, 1)
                for i in range(4):
                    mm = nc.tensor.matmul(psum[:, 6 + half, i * P:i * P + P], hT[half][:, i * P:i * P + P],
                                          wqkv_s[:, 2 * D:3 * D], start=True, stop=True)
                mm.then_inc(v_mm, 1)

            for half in range(2):
                turn_normed(0, half)
            with pe.Fori(0, NB - 1) as b:
                for half in range(2):
                    project(b, half)
                    turn_normed(b + 1, half)
            for half in range(2):
                project(NB - 1, half)

            def query_unit(n, buf, u, fresh):
                if not fresh:
                    pe.wait_ge(maxed, n * NQU + u - 1)
                hp, kind = divmod(u, len(QUNITS))
                for e in range(2):
                    h = 2 * hp + e
                    for i, k0, w, col, _ in QUNITS[kind]:
                        diag = k0 + w == (i + 1) * P
                        o = psum[:, QB[u % 2] + e, :]
                        mm = nc.tensor.matmul(o[:, col:col + w], qst[buf][0:96, h, i * P:i * P + P],
                                              kst[buf][0:96, h, k0:k0 + w], start=True, stop=not diag)
                        if diag:
                            mm = nc.tensor.matmul(o[:, col + w - P:col + w], identb[:], cmask[:],
                                                  start=False, stop=True)
                mm.then_inc(q_scores, 1)

            def max_rows(n):
                pe.wait_ge(m_step, (n + 1) * 5)
                nc.tensor.transpose(psum[:, MISC, :].bitcast(BF16)[0:96, 0:P],
                                    mparts[:].rearrange("p a h i -> p (a h i)"), identb[:]).then_inc(mT_mm, 1)

            def key_unit(n, buf, s, fresh):
                if not fresh:
                    pe.wait_ge(exped, n * NKU + s - 1)
                kind, h = divmod(s, GH)
                for kb, qc, q0, w, col in KUNITS[kind]:
                    mm = nc.tensor.matmul(psum[:, KB[s % 2], col:col + w], kst[buf][:, h, kb * P:kb * P + P],
                                          qst[buf][:, h, qc * 512 + q0:qc * 512 + q0 + w], start=True, stop=True)
                mm.then_inc(k_scores, 1)

            def values(n, buf, kind):
                if MASKED[kind]:
                    pe.wait_ge(masked, n * NMASK + masks_before(kind) + 1)
                else:
                    pe.wait_ge(exped, n * NKU + GH * kind + GH)
                pieces = [(kind, p) for p in KUNITS[kind] if not (kind == 2 and p[1] == 1)]
                if kind == 3:
                    pieces += [(2, KUNITS[2][1])]
                for k, (kb, qc, q0, w, col) in pieces:
                    for h in range(GH):
                        mm = nc.tensor.matmul(psum[32 * h:32 * h + 32, PV, q0:q0 + w], vst[buf][:, kb, h, :],
                                              probs[k % NP][:, h, col:col + w],
                                              start=kind in (0, 3) and k == kind, stop=False, skip_group_check=True)
                mm.then_inc(pv_done, 1)

            def turn(count, chunk):
                pe.wait_ge(o_copied, count)
                for i in range(4):
                    mm = nc.tensor.transpose(psum[:, MISC, i * P:i * P + P], osb[chunk][:, i * P:i * P + P], identf[:])
                mm.then_inc(oT_mm, 1)

            def turn_y(b, half, bank):
                pe.wait_ge(y_cont, b * 2 + half + 1)
                for i in range(4):
                    mm = nc.tensor.transpose(psum[:, bank, i * P:i * P + P], yc[half][:, i, :], identf[:])
                mm.then_inc(yT_mm, 1)

            def project_out(b, half, bank):
                pe.wait_ge(yT_ready, b * 2 + half + 1)
                for i in range(4):
                    mm = nc.tensor.matmul(psum[:, bank, i * P:i * P + P], yT[half][:, i * P:i * P + P],
                                          wog[:, bass.ds(b, 1), :].rearrange("p b d -> p (b d)"),
                                          start=True, stop=True)
                mm.then_inc(proj_mm, 1)

            def turn_h2(b, half, bank):
                pe.wait_ge(h2_ready, b * 2 + half + 1)
                for i in range(4):
                    mm = nc.tensor.transpose(psum[:, bank, i * P:i * P + P], rows[:, 0, 4 * half + i, 0:D], identf[:])
                mm.then_inc(h2T_mm, 1)

            def route_logits(b, bank):
                pe.wait_ge(h2T_ready, b * 2 + 2)
                for t in range(BT):
                    half, i = divmod(t, 4)
                    mm = nc.tensor.matmul(psum[:, bank, t * NE:t * NE + NE], h2T[half][:, i * P:i * P + P],
                                          rT_s[:], start=True, stop=True)
                mm.then_inc(logit_mm, 1)

            def prefix_counts(b, bank):
                pe.wait_ge(chosen, b + 1)
                m = maskbb[:].rearrange("p e t -> p (e t)")
                nc.tensor.matmul(psum[:, bank, 0:64], before[:], m, start=True, stop=True)
                nc.tensor.matmul(psum[:, bank, 64:128], onesb[:], m, start=True, stop=True).then_inc(prefix_mm, 1)

            def group(b, m, first, last, mix):
                n = b * NG + m
                nxt = (m + 1) % NG
                p = b - 1
                if not last:
                    pe.wait_ge(staged[nxt], (b + (m + 1) // NG) * 144 + 144)
                    for u in range(2):
                        query_unit(n + 1, nxt, u, False)
                pe.wait_ge(m_rows, n * 48 + 48)
                pe.wait_ge(v_staged, n + 5)
                for s in range(NKU):
                    key_unit(n, m, s, first and s < 2)
                    if not last:
                        for u in range(NQU):
                            if QSTEP[u] == s:
                                query_unit(n + 1, nxt, u, False)
                    if mix and s == 2 and m == 1:
                        pe.wait_ge(mT_copied, n + 1)
                        project_out(p, 0, MISC)
                    if mix and s == 2 and m == 2:
                        pe.wait_ge(mT_copied, n + 1)
                        turn_h2(p, 1, MISC)
                    if s == 3 and not first:
                        values(n - 1, (m + 1) % 2, 8)
                    if mix and s == 5 and m == 3:
                        pe.wait_ge(mT_copied, n + 1)
                        prefix_counts(p, MISC)
                    if s == 9 and not first:
                        if not mix or m == 0:
                            pe.wait_ge(mT_copied, n + 1)
                        elif m == 1:
                            pe.wait_ge(x1_ready, p * 2 + 1)
                        elif m == 2:
                            pe.wait_ge(h2T_ready, p * 2 + 2)
                        else:
                            pe.wait_ge(prefix_read, p + 1)
                        turn(2 * n, 1)
                    if s % 4 == 3 and s >= 7:
                        kind = s // 4 - 1
                        if kind == 0:
                            after(pe, o_copied, 2 * n)
                        if kind == 3:
                            pe.wait_ge(o_copied, 2 * n + 1)
                        values(n, m % 2, kind)
                    if mix and s == 17 and m == 0:
                        pe.wait_ge(o_norm, 2 * n)
                        turn_y(p, 0, MISC)
                    if mix and s == 14 and m == 1:
                        pe.wait_ge(o_norm, 2 * n)
                        project_out(p, 1, MISC)
                    if mix and s == 14 and m == 2:
                        pe.wait_ge(o_norm, 2 * n)
                        route_logits(p, MISC)
                    if s == 22:
                        if mix and m == 0:
                            pe.wait_ge(yT_ready, p * 2 + 1)
                        elif mix and m == 1:
                            pe.wait_ge(x1_ready, p * 2 + 2)
                        elif mix and m == 2:
                            pe.wait_ge(logit_ready, p + 1)
                        else:
                            after(pe, o_norm, 2 * n)
                        turn(2 * n + 1, 0)
                    if mix and s == 26 and m == 0:
                        pe.wait_ge(o_norm, 2 * n + 1)
                        turn_y(p, 1, MISC)
                    if mix and s == 26 and m == 1:
                        pe.wait_ge(o_norm, 2 * n + 1)
                        turn_h2(p, 0, MISC)
                    if s == MSTEP and not last:
                        if mix and m == 0:
                            pe.wait_ge(yT_ready, p * 2 + 2)
                        elif mix and m == 1:
                            pe.wait_ge(h2T_ready, p * 2 + 1)
                        else:
                            pe.wait_ge(o_norm, 2 * n + 1)
                        max_rows(n + 1)

            pe.wait_ge(part_res, 4 * NB)
            pe.wait_ge(v_ready, 2 * NB)
            pe.wait_ge(staged[0], 144)
            pe.wait_ge(stacks_clear, 2 * NG)
            for u in range(NQU):
                query_unit(0, 0, u, u < 2)
            max_rows(0)
            pe.wait_ge(stacks_clear, 3 * NG)
            for m in range(NG):
                group(0, m, m == 0, False, False)
            with pe.Fori(1, NB - 1) as b:
                for m in range(NG):
                    group(b, m, False, False, True)
            for m in range(NG):
                group(NB - 1, m, False, m == NG - 1, True)
            values(NN - 1, (NN - 1) % 2, 8)
            pe.wait_ge(o_norm, 2 * NN - 1)
            turn(2 * NN, 1)

            pe.wait_ge(o_norm, 2 * NN)
            pe.wait_ge(exped, NN * NKU)
            for half in range(2):
                turn_y(NB - 1, half, half)
            for half in range(2):
                project_out(NB - 1, half, 2 + half)
            for half in range(2):
                turn_h2(NB - 1, half, 4 + half)
            route_logits(NB - 1, PV)
            prefix_counts(NB - 1, MISC)

            pe.wait_ge(redo_ready, 1)
            again = pe.value_load(redo[0:1, 0:1], min_val=0, max_val=1)
            with pe.If(again > 0):
                with pe.Fori(0, 30) as i:
                    pe.wait_ge(bis_part, i + 1)
                    nc.tensor.matmul(psum[:, 0, 0:NE], onesb[:], part8[:], start=True, stop=True).then_inc(bis_count, 1)
                pe.wait_ge(above_part, 1)
                nc.tensor.matmul(psum[:, 3, 0:NE], onesb[:], part8[:], start=True, stop=True).then_inc(above_mm, 1)
                for k in range(2):
                    pe.wait_ge(redo_prefix_in, k + 1)
                    m = maskb[:].rearrange("p e t -> p (e t)")
                    nc.tensor.matmul(psum[:, 1 + k, 0:256], before[:], m, start=True, stop=True)
                    nc.tensor.matmul(psum[:, 1 + k, 256:512], onesb[:], m, start=True, stop=True
                                     ).then_inc(redo_prefix_mm, 1)

            CH = ((0, 4), (4, 4), (8, 2))

            def turn_rows(e, k, q):
                pe.wait_ge(rows_in[q], k * 16 + 16)
                for n, (s0, ns) in enumerate(CH):
                    if n == 2:
                        pe.wait_ge(rT_ready, e * 3 + 1)
                    elif n == 0 and not (isinstance(e, int) and e == 0):
                        pe.wait_ge(rT_ready, e * 3)
                    for i in range(ns):
                        mm = nc.tensor.transpose(psum[:, n % 2, i * P:i * P + P], xr[q][:, s0 + i, 0:D], identf[:])
                    mm.then_inc(rT_mm, 1)

            def up(e, q, n):
                s0, ns = CH[n]
                for f in range(FC):
                    k = (e * 3 + n) * FC + f
                    if not (isinstance(k, int) and k < 2):
                        pe.wait_ge(hid_ready, k - 1)
                    for j, w in enumerate((w1_s[q], wg_s[q])):
                        mm = nc.tensor.matmul(psum[:, 2 + 2 * (f % 2) + j, 0:ns * P], w[:, f * P:f * P + P],
                                              xT[q][:, s0 * P:(s0 + ns) * P], start=True, stop=True)
                    mm.then_inc(up_mm, 1)

            def down(e, q, n, par):
                s0, ns = CH[n]
                pe.wait_ge(hid_ready, (e * 3 + n) * FC + FC)
                if not (isinstance(e, int) and e * 3 + n < 2):
                    pe.wait_ge(y_ready, e * 3 + n - 1)
                for i in range(ns):
                    for f in range(FC):
                        mm = nc.tensor.matmul(psum[:, 6 + par, i * P:i * P + P], hid[par][:, f, i * P:i * P + P],
                                              w2_s[q][:, f, :], start=f == 0, stop=f == FC - 1)
                mm.then_inc(down_mm, 1)

            def expert(j, q, par, last):
                e = j * 2 + q
                k = j
                pe.wait_ge(weights_in[q], k * 48 + 48)
                pe.wait_ge(rT_ready, e * 3 + 3)
                up(e, q, 0)
                up(e, q, 1)
                down(e, q, 0, par)
                up(e, q, 2)
                down(e, q, 1, 1 - par)
                if not last:
                    turn_rows(e + 1, j + (q + 1) // 2, 1 - q)
                down(e, q, 2, par)

            turn_rows(0, 0, 0)
            expert(0, 0, 0, False)
            expert(0, 1, 1, False)
            with pe.Fori(1, 3) as j:
                expert(j, 0, 0, False)
                expert(j, 1, 1, False)
            expert(3, 0, 0, False)
            expert(3, 1, 1, True)

        @block.scalar
        def _(act):
            act.wait_ge(wmod_in, 32)
            nc.scalar.activation(et[:], ct[:], ACT.Exp, scale=-1.0).then_inc(exp_c, 1)
            for i in range(NG):
                nc.scalar.memzero(stack[:, 2048 * i:2048 * i + 2048]).then_inc(stacks_clear, 1)
            for b in range(NB):
                act.wait_ge(modrow_mm, b + 1)
                nc.scalar.activation(modrow[:, b, 0:2, :], psum[:, b, 0:256], ACT.Copy).then_inc(modrow_copied, 1)
                nc.scalar.activation(modrow[:, b, 2:4, :], psum[:, b, 256:512], ACT.Copy).then_inc(modrow_copied, 1)

            act.wait_ge(modcol_ready, 2)

            def modulate(b, half):
                act.wait_ge(xT_mm, b * 2 + half + 1)
                act.sem_inc(act_waited, 1)
                nc.scalar.activation(hT[half][:], psum[:, half, :], ACT.Identity,
                                     bias=modcol[:, 0, bass.ds(b, 1)], scale=modcol[:, 1, bass.ds(b, 1)]
                                     ).then_inc(hT_ready, 1)

            def high_parts(b, half):
                c = b * 2 + half
                for j in range(2):
                    act.wait_ge(qk_mm, c * 2 + j + 1)
                    if j == 0:
                        act.wait_ge(parts_out[half], b * 96 + 1)
                    nc.scalar.activation(parts[half][j][:, 0, :], psum[:, 2 + 2 * j + half, :], ACT.Identity,
                                         bias=bqkv_s[:, j:j + 1]).then_inc(part_hi, 1)

            def middle_parts(b, half):
                for j in range(2):
                    act.wait_ge(part_res, b * 4 + 2 * half + j + 1)
                    nc.scalar.activation(parts[half][j][:, 1, :], pres[half][j], ACT.Copy).then_inc(part_mid, 1)

            for half in range(2):
                modulate(0, half)
            with act.Fori(0, NB - 1) as b:
                for half in range(2):
                    high_parts(b, half)
                    middle_parts(b, half)
                    modulate(b + 1, half)
            for half in range(2):
                high_parts(NB - 1, half)
                middle_parts(NB - 1, half)

            def max_copy(n):
                act.wait_ge(mT_mm, n + 1)
                if not (isinstance(n, int) and n == 0):
                    act.wait_ge(m_rows, n * 48)
                nc.scalar.activation(mT[:], psum[:, MISC, :].bitcast(BF16)[0:96, 0:P], ACT.Copy
                                     ).then_inc(mT_copied, 1)

            def out_copy(count, chunk, turned):
                act.wait_ge(pv_done, count)
                after(act, oT_mm, turned)
                nc.scalar.activation(osb[chunk][:], psum[:, PV, :], ACT.Copy).then_inc(o_copied, 1)

            def y_out(b, half, bank):
                act.wait_ge(yT_mm, b * 2 + half + 1)
                nc.scalar.activation(yT[half][:], psum[:, bank, :], ACT.Copy).then_inc(yT_ready, 1)

            def h2_out(b, half, bank):
                act.wait_ge(h2T_mm, b * 2 + half + 1)
                nc.scalar.activation(h2T[half], psum[:, bank, :], ACT.Copy).then_inc(h2T_ready, 1)

            def logits_exp(b):
                act.wait_ge(lg_shifted, b + 1)
                act.sem_inc(act_waited, 1)
                nc.scalar.activation(lg[:], lg[:], ACT.Exp).then_inc(exp_l, 1)

            def group(b, m, first, last, mix):
                n = b * NG + m
                for s in range(NKU):
                    kind, h = divmod(s, GH)
                    if h == 0:
                        if kind >= NP:
                            act.wait_ge(pv_done, n * NK + (4 if kind == 5 else kind - 2))
                        elif not first:
                            act.wait_ge(pv_done, n * NK + kind - 2)
                    act.wait_ge(k_scores, n * NKU + s + 1)
                    nc.scalar.activation(probs[kind % NP][:, h, :], psum[:, KB[s % 2], :], ACT.Exp,
                                         scale=SCALE).then_inc(exped, 1)
                    if s == 5 and not first:
                        out_copy(n * NK, 1, n * 2 - 2)
                    if s == 17:
                        out_copy(n * NK + 3, 0, n * 2 - 1)
                    if mix and m == 0 and s in (18, 27):
                        y_out(b - 1, s // 27, MISC)
                    if mix and m == 1 and s == 27:
                        h2_out(b - 1, 0, MISC)
                    if mix and m == 2 and s == 3:
                        h2_out(b - 1, 1, MISC)
                    if mix and m == 2 and s == 20:
                        logits_exp(b - 1)
                    if s == MSTEP and not last:
                        max_copy(n + 1)

            max_copy(0)
            for m in range(NG):
                group(0, m, m == 0, False, False)
            with act.Fori(1, NB - 1) as b:
                for m in range(NG):
                    group(b, m, False, False, True)
            for m in range(NG):
                group(NB - 1, m, False, m == NG - 1, True)
            out_copy(NN * NK, 1, NN * 2 - 2)

            for half in range(2):
                y_out(NB - 1, half, half)
            for half in range(2):
                h2_out(NB - 1, half, 4 + half)
            logits_exp(NB - 1)

            def rows_out(e, q):
                for n, (s0, ns) in enumerate(((0, 4), (4, 4), (8, 2))):
                    act.wait_ge(rT_mm, e * 3 + n + 1)
                    nc.scalar.activation(xT[q][:, s0 * P:(s0 + ns) * P], psum[:, n % 2, 0:ns * P], ACT.Copy
                                         ).then_inc(rT_ready, 1)

            def silu(e, n, ns):
                for f in range(FC):
                    k = (e * 3 + n) * FC + f
                    if not (isinstance(k, int) and k < 2):
                        act.wait_ge(hid_ready, k - 1)
                    act.wait_ge(up_mm, k + 1)
                    nc.scalar.activation(sg[f % 2][:, 0:ns * P], psum[:, 3 + 2 * (f % 2), 0:ns * P], ACT.Silu
                                         ).then_inc(silu_ready, 1)

            def expert(j, q, last):
                e = j * 2 + q
                silu(e, 0, 4)
                silu(e, 1, 4)
                silu(e, 2, 2)
                if not last:
                    rows_out(e + 1, 1 - q)

            rows_out(0, 0)
            expert(0, 0, False)
            expert(0, 1, False)
            with act.Fori(1, 3) as j:
                expert(j, 0, False)
                expert(j, 1, False)
            expert(3, 0, False)
            expert(3, 1, True)

            for t in range(NT):
                if t % BT == 0:
                    act.wait_ge(res_in[t // BT], 32)
                nc.scalar.activation(g1[:, t, :], g1[:, t, :], ACT.Copy, scale=kw1[:, t:t + 1]).then_inc(scaled, 1)

        @block.vector
        def _(dve):
            dve.wait_ge(exp_c, 1)
            nc.vector.tensor_scalar(et[:], et[:], 1.0, None, ALU.add).then_inc(one_c, 1)
            dve.wait_ge(one_c, 1)
            nc.vector.reciprocal(et[:], et[:]).then_inc(rec_c, 1)
            dve.wait_ge(rec_c, 1)
            nc.vector.tensor_tensor(sc[:], ct[:], et[:], ALU.mult).then_inc(silu_c, 1)
            dve.wait_ge(silu_c, 1)
            nc.vector.tensor_copy(scb[:], sc[:].unsqueeze(2).to_broadcast([P, NB, P])).then_inc(wide_c, 1)
            dve.wait_ge(modcol_mm, 1)
            nc.vector.tensor_copy(modcol[:, 0, :], psum[:, MISC, 0:NB]).then_inc(modcol_ready, 1)
            nc.vector.tensor_scalar(modcol[:, 1, :], psum[:, MISC, NB:2 * NB], 1.0, None, ALU.add
                                    ).then_inc(modcol_ready, 1)

            def first_stats(b):
                for t in range(BT):
                    ins = nc.vector.bn_stats(stats[:, t, :], xs[:, bass.ds(b * BT + t, 1), :])
                ins.then_inc(ln_stats, 1)
                dve.wait_ge(ln_stats, b + 1)
                dve.sem_inc(dve_waited, 1)
                for t in range(BT):
                    ins = nc.vector.bn_aggr(mv[:, t, :], stats[:, t, :])
                ins.then_inc(ln_aggr, 1)
                dve.wait_ge(ln_aggr, b + 1)
                nc.vector.tensor_scalar(vpe[:], mv[:, :, 1], EPS_LN, None, ALU.add).then_inc(ln_eps, 1)

            def normalise(b, half):
                c = b * 2 + half
                after(dve, xT_mm, c - 1)
                if half == 0:
                    dve.wait_ge(ln_rstd, b + 1)
                for i in range(4):
                    k = 4 * half + i
                    ins = nc.vector.tensor_scalar(xn[half][:, i, :], xs[:, bass.ds(c * 4 + i, 1), :],
                                                  mv[:, k:k + 1, 0], rstd[:, k:k + 1], ALU.subtract, ALU.mult)
                ins.then_inc(ln_norm, 1)

            def residues(b, half):
                c = b * 2 + half
                for j in range(2):
                    dve.wait_ge(part_hi, c * 2 + j + 1)
                    nc.vector.scalar_tensor_tensor(out=pres[half][j], in0=psum[:, 2 + 2 * j + half, :],
                                                   scalar=bqkv_s[:, j:j + 1], in1=parts[half][j][:, 0, :],
                                                   op0=ALU.add, op1=ALU.subtract).then_inc(part_res, 1)
                dve.wait_ge(v_mm, c + 1)
                nc.vector.tensor_tensor(
                    vals[:, bass.ds(b * NG, NG), 4 * half:4 * half + 4, :].rearrange("p g t d -> p t g d"),
                    psum[:, 6 + half, :].rearrange("p (t g d) -> p t g d", t=4, g=NG),
                    bv_row[:].rearrange("p (a g d) -> p a g d", a=1, g=NG).to_broadcast([P, 4, NG, 32]),
                    ALU.add).then_inc(v_ready, 1)

            dve.wait_ge(x_in[0], 16)
            first_stats(0)
            normalise(0, 0)
            normalise(0, 1)
            g = modrow[:, :, 0:4:3, :]
            dve.wait_ge(modrow_copied, 2 * NB)
            nc.vector.tensor_scalar(modrow[:, :, 2, :], modrow[:, :, 2, :], 1.0, None, ALU.add).then_inc(gates_ready, 1)
            nc.vector.tensor_scalar(gneg[:], g, -1.0, 0.25, ALU.mult, ALU.max).then_inc(gates_ready, 1)
            nc.vector.tensor_scalar(gsgn[:], g, 0.0, 2.0, ALU.is_ge, ALU.mult).then_inc(gates_ready, 1)
            dve.wait_ge(gates_ready, 3)
            nc.vector.tensor_tensor(gneg[:], gneg[:], g, ALU.max).then_inc(gates_ready, 1)
            dve.wait_ge(gates_ready, 4)
            for a in range(2):
                nc.vector.scalar_tensor_tensor(out=modrow[:, :, 3 * a, :], in0=gsgn[:, :, a, :], scalar=-1.0,
                                               in1=gneg[:, :, a, :], op0=ALU.add, op1=ALU.mult
                                               ).then_inc(gates_ready, 1)
            dve.wait_ge(w_in, 96)
            for q in range(1, 4):
                dve.wait_ge(x_in[q], 16)
            with dve.Fori(0, NB - 1) as b:
                first_stats(b + 1)
                for half in range(2):
                    residues(b, half)
                    normalise(b + 1, half)
            for half in range(2):
                residues(NB - 1, half)

            def maximum(n, u):
                dve.wait_ge(q_scores, n * NQU + u + 1)
                hp, kind = divmod(u, len(QUNITS))
                for i, k0, w, col, part in QUNITS[kind]:
                    ins = nc.vector.tensor_reduce(mx[:, part, 2 * hp:2 * hp + 2, i],
                                                  psum[:, QB[u % 2]:QB[u % 2] + 2, col:col + w], AX.X, ALU.max)
                ins.then_inc(maxed, 1)

            def negated_parts(n, first):
                k = n * 5
                dve.wait_ge(maxed, (n + 1) * NQU)
                if not first:
                    dve.wait_ge(mT_mm, n)
                nc.vector.tensor_tensor(mx[:, 0, :, 4:8], mx[:, 0, :, 4:8], mx[:, 1, :, 4:8], ALU.max
                                        ).then_inc(m_step, 1)
                dve.wait_ge(m_step, k + 1)
                nc.vector.tensor_scalar(mparts[:, 0, :, :], mx[:, 0, :, :], -1.0, None, ALU.mult).then_inc(m_step, 1)
                dve.wait_ge(m_step, k + 2)
                nc.vector.scalar_tensor_tensor(out=mres[:], in0=mx[:, 0, :, :], scalar=-1.0, in1=mparts[:, 0, :, :],
                                               op0=ALU.mult, op1=ALU.subtract).then_inc(m_step, 1)
                dve.wait_ge(m_step, k + 3)
                nc.vector.tensor_copy(mparts[:, 1, :, :], mres[:]).then_inc(m_step, 1)
                dve.wait_ge(m_step, k + 4)
                nc.vector.tensor_tensor(mparts[:, 2, :, :], mres[:], mparts[:, 1, :, :], ALU.subtract
                                        ).then_inc(m_step, 1)

            def normed(count, n, chunk):
                dve.wait_ge(oT_mm, count)
                o = psum[:, MISC, :].rearrange("p (t h d) -> p t h d", t=4, h=GH)
                nc.vector.reciprocal(rec[:].unsqueeze(3), o[:, :, :, HD:HD + 1]).then_inc(o_rec, 1)
                dve.wait_ge(o_rec, count)
                nc.vector.tensor_tensor(
                    ys[:, bass.ds(n, 1), 4 * chunk:4 * chunk + 4, :].rearrange("p n t (h d) -> p (n t) h d", h=GH),
                    o[:, :, :, 0:HD], rec[:].unsqueeze(3).to_broadcast([P, 4, GH, HD]),
                    ALU.mult).then_inc(o_norm, 1)

            rev_b = rev[:, 0:1, :].to_broadcast([P, BT, NE])

            def add_attention(b, half, bank):
                c = b * 2 + half
                dve.wait_ge(bias_in, c + 1)
                dve.wait_ge(proj_mm, c + 1)
                xv = xs[:, bass.ds(c * 4, 4), :]
                nc.vector.tensor_tensor(xv, psum[:, bank, :].rearrange("p (t d) -> p t d", t=4), xv,
                                        ALU.add).then_inc(x1_ready, 1)

            def second_stats(b, half):
                c = b * 2 + half
                dve.wait_ge(x1_ready, c + 1)
                dve.sem_inc(dve_waited, 1)
                for i in range(4):
                    ins = nc.vector.bn_stats(stats2[half][:, i, :], xs[:, bass.ds(c * 4 + i, 1), :])
                ins.then_inc(n2_stats, 1)
                dve.wait_ge(n2_stats, c + 1)
                dve.sem_inc(dve_waited, 1)
                for i in range(4):
                    ins = nc.vector.bn_aggr(mv2[half][:, i, :], stats2[half][:, i, :])
                ins.then_inc(n2_aggr, 1)
                dve.wait_ge(n2_aggr, c + 1)
                nc.vector.tensor_scalar(vpe2[half][:], mv2[half][:, :, 1], EPS_LN, None, ALU.add
                                        ).then_inc(n2_step, 1)

            STEPS = 26
            steps = [0]

            def then(b, ins):
                steps[0] += 1
                ins.then_inc(route_step, 1)
                dve.wait_ge(route_step, b * STEPS + steps[0])

            def te(v, t=BT):
                return v.unsqueeze(2).to_broadcast([P, t, NE])

            def perm(v):
                return v.rearrange("p e t -> p t e")

            def shifted_logits(b, bank):
                steps[0] = 0
                dve.wait_ge(logit_mm, b + 1)
                nc.vector.tensor_copy(lg[:], psum[:, bank, 0:BT * NE].rearrange("p (t e) -> p t e", t=BT)
                                      ).then_inc(logit_ready, 1)
                dve.wait_ge(logit_ready, b + 1)
                then(b, nc.vector.tensor_reduce(m1b, lg[:], AX.X, ALU.max))
                nc.vector.tensor_tensor(lg[:], lg[:], te(m1b), ALU.subtract).then_inc(lg_shifted, 1)

            def first_choice(b):
                dve.wait_ge(exp_l, b + 1)
                then(b, nc.vector.tensor_reduce(smb, lg[:], AX.X, ALU.add))
                then(b, nc.vector.reciprocal(smb, smb))
                then(b, nc.vector.tensor_tensor(pr[:], lg[:], te(smb), ALU.mult))
                pm = pm1[:, bass.ds(b * BT, BT)]
                then(b, nc.vector.tensor_reduce(pm, pr[:], AX.X, ALU.max))
                then(b, nc.vector.tensor_tensor(eqb[:], pr[:], te(pm), ALU.is_equal))
                then(b, nc.vector.tensor_tensor(tvb[:], eqb[:], rev_b, ALU.mult))
                then(b, nc.vector.tensor_reduce(first1b, tvb[:], AX.X, ALU.max))
                then(b, nc.vector.tensor_tensor(oh1[:, bass.ds(b * BT, BT), :], rev_b, te(first1b), ALU.is_equal))

            def second_choice(b):
                pm = pm2[:, bass.ds(b * BT, BT)]
                one, two = (v[:, bass.ds(b * BT, BT), :] for v in (oh1, oh2))
                then(b, nc.vector.scalar_tensor_tensor(out=pr[:], in0=one, scalar=-2.0, in1=pr[:], op0=ALU.mult,
                                                       op1=ALU.add))
                then(b, nc.vector.tensor_reduce(pm, pr[:], AX.X, ALU.max))
                then(b, nc.vector.tensor_tensor(eqb[:], pr[:], te(pm), ALU.is_equal))
                then(b, nc.vector.tensor_tensor(tvb[:], eqb[:], rev_b, ALU.mult))
                then(b, nc.vector.tensor_reduce(first2b, tvb[:], AX.X, ALU.max))
                then(b, nc.vector.tensor_tensor(two, rev_b, te(first2b), ALU.is_equal))
                nc.vector.tensor_tensor(perm(maskbb[:]), one, two, ALU.add).then_inc(chosen, 1)

            def ranks(b, bank):
                dve.wait_ge(prefix_mm, b + 1)
                flat = [v[:].rearrange("p e t -> p (e t)") for v in (scanb, exclb, rankb)]
                tot = psum[:, bank, 64:128]
                then(b, nc.vector.tensor_tensor_scan(flat[0], onesf[:, 0:64], tot, 0.0, ALU.mult, ALU.add))
                then(b, nc.vector.tensor_tensor(flat[1], flat[0], tot, ALU.subtract))
                nc.vector.tensor_tensor(flat[2], psum[:, bank, 0:64], flat[1], ALU.add).then_inc(prefix_read, 1)
                then(b, nc.vector.tensor_tensor(shift[:], used[:], exclb[:, :, 0], ALU.subtract))
                dve.wait_ge(prefix_read, b + 1)
                then(b, nc.vector.tensor_tensor(rankb[:], rankb[:],
                                                shift[:].unsqueeze(2).to_broadcast([P, NE, BT]), ALU.add))
                nc.vector.tensor_tensor(used[:], shift[:], scanb[:, :, BT - 1], ALU.add)

            def slots(b):
                then(b, nc.vector.tensor_scalar(overb[:], rankb[:], float(CAP), FAR, ALU.is_ge, ALU.mult))
                then(b, nc.vector.tensor_tensor(overb[:], overb[:], rankb[:], ALU.add))
                then(b, nc.vector.tensor_tensor(overb[:], overb[:],
                                                rev[:, 1, :].unsqueeze(2).to_broadcast([P, NE, BT]), ALU.add))
                for k, (oh, tmp, sl) in enumerate(((oh1, eqb, first1b), (oh2, tvb, first2b))):
                    then(b, nc.vector.tensor_tensor(tmp[:], oh[:, bass.ds(b * BT, BT), :], perm(overb[:]), ALU.mult))
                    then(b, nc.vector.tensor_reduce(sl, tmp[:], AX.X, ALU.add))
                    nc.vector.tensor_copy(idxb[:, k, :], sl).then_inc(idx_ready, 1)
                assert steps[0] == STEPS

            def group(b, m, first, last, mix):
                n = b * NG + m
                p = b - 1
                for s in range(-1, NKU):
                    if not last:
                        for u in range(NQU):
                            if QSTEP[u] == s:
                                maximum(n + 1, u)
                    if mix and m == 3 and s == 6:
                        ranks(p, MISC)
                    if s == 11 and not first:
                        normed(n * 2, n - 1, 1)
                    if s == 24:
                        normed(n * 2 + 1, n, 0)
                    if mix and m == 1 and s in (4, 16):
                        add_attention(p, s // 16, MISC)
                        second_stats(p, s // 16)
                    if mix and m == 2 and s == 16:
                        shifted_logits(p, MISC)
                    if mix and m == 2 and s == 24:
                        first_choice(p)
                    if mix and m == 3 and s == 2:
                        second_choice(p)
                    if mix and m == 3 and s == 8:
                        slots(p)
                if not last:
                    negated_parts(n + 1, False)

            for u in range(NQU):
                maximum(0, u)
            negated_parts(0, True)
            dve.wait_ge(iotas, 5)
            for i in range(2):
                nc.vector.tensor_copy(rev[:, i, :], rev_i[:, i, :]).then_inc(rev_ready, 1)
            dve.wait_ge(rev_ready, 2)
            for m in range(NG):
                group(0, m, m == 0, False, False)
            with dve.Fori(1, NB - 1) as b:
                for m in range(NG):
                    group(b, m, False, False, True)
            for m in range(NG):
                group(NB - 1, m, False, m == NG - 1, True)
            normed(NN * 2, NN - 1, 1)

            b = NB - 1
            for half in range(2):
                add_attention(b, half, 2 + half)
            for half in range(2):
                second_stats(b, half)
            shifted_logits(b, PV)
            first_choice(b)
            second_choice(b)
            ranks(b, MISC)
            dve.wait_ge(prefix_mm, NB)
            slots(b)

            last_steps = [0]

            def finish(ins):
                last_steps[0] += 1
                ins.then_inc(last_step, 1)
                dve.wait_ge(last_step, last_steps[0])

            finish(nc.vector.tensor_scalar(acc[:], used[:], float(CAP), None, ALU.is_gt))
            nc.vector.tensor_reduce(redo[:], acc[:], AX.X, ALU.max).then_inc(redo_ready, 1)
            finish(nc.vector.tensor_tensor(sm, pm1, pm2, ALU.add))
            finish(nc.vector.tensor_scalar(sm, sm, EPS, None, ALU.max))
            finish(nc.vector.reciprocal(sm, sm))
            nc.vector.tensor_tensor(w1s, pm1, sm, ALU.mult)
            finish(nc.vector.tensor_tensor(w2s, pm2, sm, ALU.mult))

            redo_steps = [0]

            def again_then(ins):
                redo_steps[0] += 1
                ins.then_inc(redo_step, 1)
                dve.wait_ge(redo_step, redo_steps[0])

            def counted(src, threshold, op):
                nc.vector.tensor_tensor(cmp_, src, threshold.unsqueeze(2).to_broadcast([P, NE, NT]), op
                                        ).then_inc(bis_step, 1)

            def prefix(k):
                dve.wait_ge(redo_prefix_mm, k + 1)
                tot = psum[:, 1 + k, 256:512]
                flat = [v.rearrange("p e t -> p (e t)") for v in (scan1, excl, rank)]
                again_then(nc.vector.tensor_tensor_scan(flat[0], onesf[:], tot, 0.0, ALU.mult, ALU.add))
                again_then(nc.vector.tensor_tensor(flat[1], tot, flat[0], ALU.subtract))
                again_then(nc.vector.tensor_tensor(rank, excl[:, :, 0:1].to_broadcast([P, NE, NT]), excl, ALU.subtract))
                again_then(nc.vector.tensor_tensor(flat[2], psum[:, 1 + k, 0:256], flat[2], ALU.add))

            dve.wait_ge(redo_ready, 1)
            again = dve.value_load(redo[0:1, 0:1], min_val=0, max_val=1)
            with dve.If(again > 0):
                nc.vector.tensor_tensor(wa, oh1[:], te(w1s, NT), ALU.mult)
                again_then(nc.vector.tensor_tensor(wb, oh2[:], te(w2s, NT), ALU.mult))
                nc.vector.scalar_tensor_tensor(out=eq, in0=oh1[:], scalar=-1.0, in1=oh2[:], op0=ALU.add, op1=ALU.add)
                again_then(nc.vector.tensor_tensor(wa, wa, wb, ALU.add))
                again_then(nc.vector.tensor_tensor(perm(wsel), wa, eq, ALU.add))
                nc.vector.memset(thr[:], 0)
                again_then(nc.vector.memset(bit[:], 1 << 29))
                with dve.Fori(0, 30) as i:
                    k = i * 6
                    nc.vector.tensor_tensor(cand[:], thr[:], bit[:], ALU.bitwise_or).then_inc(bis_step, 1)
                    dve.wait_ge(bis_step, k + 1)
                    counted(wsel, cand[:].bitcast(F32), ALU.is_ge)
                    dve.wait_ge(bis_step, k + 2)
                    nc.vector.tensor_reduce(acc[:], cmp_, AX.X, ALU.add).then_inc(bis_step, 1)
                    dve.wait_ge(bis_step, k + 3)
                    nc.vector.tensor_copy(part8[:], acc[:]).then_inc(bis_part, 1)
                    nc.vector.tensor_single_scalar(bit[:], bit[:], 1, ALU.logical_shift_right).then_inc(bis_step, 1)
                    dve.wait_ge(bis_count, i + 1)
                    nc.vector.scalar_tensor_tensor(out=acc[:], in0=psum[:, 0, 0:NE], scalar=float(CAP),
                                                   in1=cand[:].bitcast(F32), op0=ALU.is_ge, op1=ALU.mult
                                                   ).then_inc(bis_step, 1)
                    dve.wait_ge(bis_step, k + 5)
                    nc.vector.tensor_tensor(thr[:].bitcast(F32), thr[:].bitcast(F32), acc[:], ALU.max
                                            ).then_inc(bis_step, 1)
                    dve.wait_ge(bis_step, k + 6)
                thr_b = thr[:].bitcast(F32).unsqueeze(2).to_broadcast([P, NE, NT])
                again_then(nc.vector.tensor_tensor(keep, wsel, thr_b, ALU.is_gt))
                again_then(nc.vector.tensor_reduce(acc[:], keep, AX.X, ALU.add))
                nc.vector.tensor_copy(part8[:], acc[:]).then_inc(above_part, 1)
                again_then(nc.vector.tensor_tensor(cmp_, wsel, thr_b, ALU.is_equal))
                nc.vector.tensor_copy(maskb[:], cmp_).then_inc(redo_prefix_in, 1)
                dve.wait_ge(above_mm, 1)
                again_then(nc.vector.tensor_scalar(need[:], psum[:, 3, 0:NE], -1.0, float(CAP), ALU.mult, ALU.add))
                prefix(0)
                again_then(nc.vector.tensor_tensor(rank, rank, need[:].unsqueeze(2).to_broadcast([P, NE, NT]),
                                                   ALU.is_lt))
                again_then(nc.vector.tensor_tensor(rank, rank, cmp_, ALU.mult))
                again_then(nc.vector.tensor_tensor(keep, keep, rank, ALU.add))
                nc.vector.tensor_copy(maskb[:], keep).then_inc(redo_prefix_in, 1)
                prefix(1)
                again_then(nc.vector.tensor_tensor(rank, rank, rev[:, 1, :].unsqueeze(2).to_broadcast([P, NE, NT]),
                                                   ALU.add))
                again_then(nc.vector.tensor_scalar(rank, rank, -FAR, None, ALU.add))
                again_then(nc.vector.tensor_tensor(rank, rank, keep, ALU.mult))
                again_then(nc.vector.tensor_scalar(slot, rank, FAR, None, ALU.add))
                for k, (oh, sl, kp) in enumerate(((oh1[:], slot1, keep1), (oh2[:], slot2, keep2))):
                    again_then(nc.vector.tensor_tensor(prod, oh, perm(slot), ALU.mult))
                    again_then(nc.vector.tensor_reduce(sl, prod, AX.X, ALU.add))
                    nc.vector.tensor_copy(idx[:, k, :], sl).then_inc(redo_idx, 1)
                    again_then(nc.vector.tensor_tensor(wa, oh, perm(keep), ALU.mult))
                    again_then(nc.vector.tensor_reduce(kp, wa, AX.X, ALU.add))
            nc.vector.tensor_tensor(kw1, w1s, keep1, ALU.mult)
            finish(nc.vector.tensor_tensor(kw2, w2s, keep2, ALU.mult))
            finish(nc.vector.tensor_tensor(sm, kw1, kw2, ALU.add))
            finish(nc.vector.tensor_scalar(sm, sm, EPS, None, ALU.max))
            finish(nc.vector.reciprocal(sm, sm))
            nc.vector.tensor_tensor(kw1, kw1, sm, ALU.mult)
            finish(nc.vector.tensor_tensor(kw2, kw2, sm, ALU.mult))

            def gate(e, n, ns, par):
                for f in range(FC):
                    k = (e * 3 + n) * FC + f
                    dve.wait_ge(silu_ready, k + 1)
                    nc.vector.tensor_tensor(hid[par][:, f, 0:ns * P], psum[:, 2 + 2 * (f % 2), 0:ns * P],
                                            sg[f % 2][:, 0:ns * P], ALU.mult).then_inc(hid_ready, 1)

            def results_out(e, q, n, s0, ns, par):
                dve.wait_ge(down_mm, e * 3 + n + 1)
                nc.vector.tensor_copy(yo[q][:, s0:s0 + ns, :],
                                      psum[:, 6 + par, 0:ns * P].rearrange("p (s d) -> p s d", s=ns)
                                      ).then_inc(y_ready, 1)

            def expert(j, q, par):
                e = j * 2 + q
                gate(e, 0, 4, par)
                gate(e, 1, 4, 1 - par)
                if not isinstance(j, int):
                    dve.wait_ge(sent[q], j * (16 * ST))
                results_out(e, q, 0, 0, 4, par)
                gate(e, 2, 2, par)
                results_out(e, q, 1, 4, 4, 1 - par)
                results_out(e, q, 2, 8, 2, par)

            expert(0, 0, 0)
            expert(0, 1, 1)
            with dve.Fori(1, NE // 2) as j:
                expert(j, 0, 0)
                expert(j, 1, 1)

            for b in range(NB):
                for t in range(b * BT, b * BT + BT):
                    dve.wait_ge(scaled, t + 1)
                    ins = nc.vector.scalar_tensor_tensor(out=g1[:, t, :], in0=g2[:, t, :], scalar=kw2[:, t:t + 1],
                                                         in1=g1[:, t, :], op0=ALU.mult, op1=ALU.add)
                ins.then_inc(summed, 1)
                dve.wait_ge(summed, b + 1)
                v = g1[:, b * BT:b * BT + BT, :]
                nc.vector.tensor_tensor(v, v, modrow[:, b:b + 1, 3, :].to_broadcast([P, BT, D]), ALU.mult
                                        ).then_inc(gated, 1)
                dve.wait_ge(gated, b + 1)
                nc.vector.tensor_tensor(v, v, xs[:, b * BT:b * BT + BT, :], ALU.add).then_inc(finished, 1)


def kernel(L0_attn_x, L0_attn_w_qkv, L0_attn_b_qkv, L0_attn_w_out, L0_attn_b_out, L0_ffn_router_weight,
           L0_ffn_ff_pre_act_weight, L0_ffn_gate_weight, L0_ffn_ff_post_act_weight, L0_c, L0_wmod):
    import numpy as np
    import concourse.bacc as bacc
    from concourse.bass_utils import run_bass_kernel_spmd

    order = np.arange(D).reshape(NG, GH, HD).transpose(0, 2, 1).reshape(-1)
    w, bq = np.asarray(L0_attn_w_qkv), np.asarray(L0_attn_b_qkv)
    rows = np.concatenate([order, D + order, np.arange(2 * D, 3 * D)])

    def turned(a):
        return np.ascontiguousarray(np.swapaxes(np.asarray(a), -1, -2))

    arrays = {
        "x": np.ascontiguousarray(L0_attn_x),
        "wqkvT": turned(w[rows]),
        "bqkv": np.ascontiguousarray(bq[rows].reshape(3, D).T),
        "bv": np.ascontiguousarray(bq[2 * D:].reshape(1, D)),
        "woT": turned(L0_attn_w_out),
        "bout": np.ascontiguousarray(L0_attn_b_out).reshape(1, D),
        "rT": turned(L0_ffn_router_weight),
        "w1T": turned(L0_ffn_ff_pre_act_weight),
        "wgT": turned(L0_ffn_gate_weight),
        "w2T": turned(L0_ffn_ff_post_act_weight),
        "cT": turned(L0_c),
        "wmod": np.ascontiguousarray(L0_wmod),
    }
    nc = bacc.Bacc("TRN2", target_bir_lowering=False, num_devices=1)
    args = {n: nc.dram_tensor(n, a.shape, mybir.dt.from_np(a.dtype), kind="ExternalInput").ap()
            for n, a in arrays.items()}
    args["out"] = nc.dram_tensor("out", [NB, S, D], F32, kind="ExternalOutput").ap()
    build(nc, **args)
    return run_bass_kernel_spmd(nc, [arrays], core_ids=[0]).results[0]["out"]
```

```python
from contextlib import ExitStack

import concourse.bass as bass
from concourse import mybir

ALU = mybir.AluOpType
ACT = mybir.ActivationFunctionType
F32 = mybir.dt.float32
BF16 = mybir.dt.bfloat16
F32R = mybir.dt.float32r
I32 = mybir.dt.int32
AX = mybir.AxisListType

P = 128
NB, S, D = 4, 1024, 128
H, HD = 16, 8
GH = 4
NG = H // GH
NN = NB * NG
T = NB * S
NT = T // P
BT = S // P
NE, F = 8, 512
CAP = 1280
SLOTS = NE * CAP
ST = CAP // P
FC = F // P
CH = ((0, 4), (4, 4), (8, 2))
ROW = D + 1
EPS_LN = 1e-5
EPS = 1.1920929e-07
NEG = -1e30
FAR = 1048576.0
SCALE = float(HD) ** -0.5

QUNITS = [
    [(4, 0, 512, 0, 0)],
    [(5, 0, 512, 0, 0)],
    [(6, 0, 512, 0, 0)],
    [(7, 0, 512, 0, 0)],
    [(3, 0, 512, 0, 0)],
    [(7, 512, 512, 0, 1)],
    [(0, 0, 128, 0, 0), (6, 512, 384, 128, 1)],
    [(4, 512, 128, 0, 1), (2, 0, 384, 128, 0)],
    [(1, 0, 256, 0, 0), (5, 512, 256, 256, 1)],
]
NQU = 2 * len(QUNITS)
KUNITS = [
    [(0, 0, 0, 512, 0)],
    [(1, 0, 128, 384, 0), (3, 0, 384, 128, 384)],
    [(2, 0, 256, 256, 0), (6, 1, 256, 256, 256)],
    [(0, 1, 0, 512, 0)],
    [(1, 1, 0, 512, 0)],
    [(2, 1, 0, 512, 0)],
    [(3, 1, 0, 512, 0)],
    [(4, 1, 0, 512, 0)],
    [(5, 1, 128, 384, 0), (7, 1, 384, 128, 384)],
]
NK = len(KUNITS)
NKU = GH * NK
NP = 3


def diagonal(piece):
    kb, qc, q0, w, col = piece
    return kb * P == qc * 512 + q0


MASKED = [any(diagonal(p) for p in kind) for kind in KUNITS]
NMASK = sum(MASKED)
QSTEP = [-7 + u * 32 // NQU for u in range(NQU)]
EARLY = sum(q < 0 for q in QSTEP)
NSTEP, MSTEP = 24, 29


def after(engine, semaphore, count):
    if not (isinstance(count, int) and count <= 0):
        engine.wait_ge(semaphore, count)


def build(nc, x, wqkvT, bqkv, bv, woT, bout, rT, w1T, wgT, w2T, cT, wmod, out):
    with ExitStack() as ctx:
        def sb(name, shape, dt=F32):
            return ctx.enter_context(nc.sbuf_tensor(name, shape, dt))

        def sem(name):
            return ctx.enter_context(nc.semaphore(name))

        def dram(name, shape, dt=F32):
            return nc.dram_tensor(name, shape, dt, kind="Internal").ap()

        k_parts = dram("k_parts", [NN, 3, 32, S], BF16)
        q_parts = dram("q_parts", [NN, 3, 32, S], BF16)
        slot_rows = dram("slot_rows", [SLOTS, ROW])
        results = dram("results", [2 * T, D])

        xs = sb("xs", [P, NT, D])
        vals = sb("vals", [P, NN, BT, 32])
        ys = sb("ys", [P, NN, BT, 32])
        modrow = sb("modrow", [P, NB, 4, D])
        rT_s = sb("rT_s", [P, NE])
        wo_s = sb("wo_s", [P, D])
        bo_row = sb("bo_row", [P, D])
        identf = sb("identf", [P, P])
        identb = sb("identb", [P, P], BF16)
        cmask = sb("cmask", [P, P], BF16)
        before = sb("before", [P, P], BF16)
        onesb = sb("onesb", [P, P], BF16)
        stats = sb("stats", [P, BT, 6])
        mv = sb("mv", [P, BT, 2])
        vpe = sb("vpe", [P, BT])
        rstd = sb("rstd", [P, BT])
        mhalf = sb("mhalf", [P, BT])
        fill = sb("fill", [P, ROW])

        vst = [sb(f"vst{i}", [P, BT, GH, 32]) for i in range(2)]
        osb = [sb(f"osb{i}", [P, 512]) for i in range(2)]
        mx = sb("mx", [P, 2, GH, BT])
        mparts = sb("mparts", [P, 3, GH, BT], BF16)
        mres = sb("mres", [P, GH, BT])
        mT = sb("mT", [96, P], BF16)
        rec = sb("rec", [P, BT // 2, GH])

        wqkv_s = sb("wqkv_s", [P, 3 * D])
        bqkv_s = sb("bqkv_s", [P, 3])
        bv_row = sb("bv_row", [P, D])
        ct = sb("ct", [P, NB])
        et = sb("et", [P, NB])
        sc = sb("sc", [P, NB])
        modcol = sb("modcol", [P, 2, NB])
        xn = [sb(f"xn{i}", [P, 4, D]) for i in range(2)]
        hT = [sb(f"hT{i}", [P, 512]) for i in range(2)]
        early = sb("early", [P, 12 * 256 + 2 * BT * ROW])
        pres = [[early[:, 3072 + (2 * i + j) * 512:3584 + (2 * i + j) * 512] for j in range(2)] for i in range(2)]

        wog = sb("wog", [P, NB, D])
        gab = sb("gab", [P, NB, D])
        stats2 = [sb(f"stats2{i}", [P, 4, 6]) for i in range(2)]
        mv2 = [sb(f"mv2{i}", [P, 4, 2]) for i in range(2)]
        vpe2 = [sb(f"vpe2{i}", [P, 4]) for i in range(2)]
        rstd2 = [sb(f"rstd2{i}", [P, 4]) for i in range(2)]
        yc, yT = xn, hT
        h2T = [xn[i][:].rearrange("p t d -> p (t d)") for i in range(2)]
        rows = early[:, 3072:3072 + 2 * BT * ROW].rearrange("p (k t r) -> p k t r", k=2, t=BT)
        dests = sb("dests", [P, 2, NT], I32)
        lg, pr, eqb, tvb = (sb(f"{n}", [P, BT, NE]) for n in ("lg", "pr", "eqb", "tvb"))
        topb = sb("topb", [P, 4, BT])
        m1b, smb, first1b, first2b = (topb[:, i, :] for i in range(4))
        maskbb = sb("maskbb", [P, NE, BT], BF16)
        scanb, exclb, rankb, overb = (sb(f"{n}", [P, NE, BT]) for n in ("scanb", "exclb", "rankb", "overb"))
        used = sb("used", [P, NE])
        shift = sb("shift", [P, NE])
        idxb = sb("idxb", [P, 2, BT], I32)
        oh1, oh2 = sb("oh1", [P, NT, NE]), sb("oh2", [P, NT, NE])

        small = sb("small", [P, 11, NT])
        sm, pm1, pm2, w1s, w2s, keep1, keep2, kw1, kw2, slot1, slot2 = (small[:, i, :] for i in range(11))
        kept_rows = vals[:].rearrange("p n t d -> p (n t d)").rearrange("p (t d) -> p t d", d=D)
        idx = sb("idx", [P, 2, NT], I32)
        rev_i = sb("rev_i", [P, 2, NE], I32)
        rev = sb("rev", [P, 2, NE])
        thr = sb("thr", [P, NE], I32)
        cand = sb("cand", [P, NE], I32)
        bit = sb("bit", [P, NE], I32)
        acc = sb("acc", [P, NE])
        need = sb("need", [P, NE])
        redo = sb("redo", [P, 1], I32)
        onesf = sb("onesf", [P, NE * NT])
        part8 = sb("part8", [P, NE], BF16)
        maskb = sb("maskb", [P, NE, NT], BF16)

        w_raw = [early[:, i * 3 * F:(i + 1) * 3 * F] for i in range(2)]
        attention = ExitStack()
        stack = attention.enter_context(nc.sbuf_tensor("stack", [P, 2 * NG * GH * S // 2], F32))
        prob_all = attention.enter_context(nc.sbuf_tensor("prob_all", [P, NP * GH * 512], F32))
        stacks = [stack[:, i * 2 * S:(i + 1) * 2 * S].bitcast(BF16).rearrange("p (h q) -> p h q", h=GH)
                  for i in range(2 * NG)]
        qst, kst = stacks[:NG], stacks[NG:]
        probs = [prob_all[:, i * 2048:(i + 1) * 2048].rearrange("p (h q) -> p h q", h=GH) for i in range(NP)]
        wmod_s = prob_all[:, 0:6 * D]
        scb = prob_all[:, 768:768 + NB * P].rearrange("p (b q) -> p b q", b=NB)
        gneg = prob_all[:, 1280:1280 + 2 * NB * D].rearrange("p (b a d) -> p b a d", b=NB, a=2)
        gsgn = prob_all[:, 0:2 * NB * D].rearrange("p (b a d) -> p b a d", b=NB, a=2)
        parts = [[[room[:, (2 * i + j) * 768:(2 * i + j) * 768 + 768].bitcast(BF16)
                   .rearrange("p (a q) -> p a q", a=3) for j in range(2)] for i in range(2)]
                 for room in (early[:, 0:3072], prob_all[:, 2304:2304 + 3072])]

        tile_no = iter(range(24))

        def rt(by_expert=False):
            i = next(tile_no)
            v = prob_all[:, i * 256:(i + 1) * 256]
            return v.rearrange("p (e t) -> p e t", e=NE) if by_expert else v.rearrange("p (t e) -> p t e", e=NE)

        eq, wa, wb = (rt() for _ in range(3))
        wsel, cmp_, keep, rank, slot, scan1, excl = (rt(True) for _ in range(7))
        prod = rt()
        attention.close()
        w_h, w_l = ([sb(f"w_{n}{i}", [P, 2 * F], F32R) for i in range(2)] for n in "hl")
        x_h, x_l = ([sb(f"x_{n}{i}", [P, CAP], F32R) for i in range(2)] for n in "hl")
        flat_vals = vals[:].rearrange("p n t d -> p (n t d)")
        flat_ys = ys[:].rearrange("p n t d -> p (n t d)")
        NX = ST * ROW
        xr = [flat_vals[:, i * NX:(i + 1) * NX].rearrange("p (s r) -> p s r", s=ST) for i in range(2)]
        yo = [flat_ys[:, i * CAP:(i + 1) * CAP].rearrange("p (s d) -> p s d", s=ST) for i in range(2)]
        dest_of = [sb(f"dest_of{i}", [P, ST], I32) for i in range(2)]
        sg = [hT[i] for i in range(2)]
        hid = [sb(f"hid{i}", [P, FC, 512]) for i in range(2)]

        g1 = vals[:].rearrange("p n t d -> p (n t d)").rearrange("p (t d) -> p t d", d=D)
        g2 = ys[:].rearrange("p n t d -> p (n t d)").rearrange("p (t d) -> p t d", d=D)

        psum = ctx.enter_context(nc.psum_tensor("psum", [P, 8, 512], F32))

        x_in = [sem(f"x_in{q}") for q in range(4)]
        w_in, wmod_in = sem("w_in"), sem("wmod_in")
        consts_ready, fill_ready, filled = sem("consts_ready"), sem("fill_ready"), sem("filled")
        exp_c, one_c, rec_c, silu_c, wide_c = (sem(n) for n in ("exp_c", "one_c", "rec_c", "silu_c", "wide_c"))
        modcol_mm, modcol_ready, modrow_mm, modrow_copied = (
            sem(n) for n in ("modcol_mm", "modcol_ready", "modrow_mm", "modrow_copied"))
        gates_ready = sem("gates_ready")
        ln_stats, ln_aggr, ln_eps, ln_rstd, ln_norm = (
            sem(n) for n in ("ln_stats", "ln_aggr", "ln_eps", "ln_rstd", "ln_norm"))
        xT_mm, hT_ready, qk_mm, v_mm = (sem(n) for n in ("xT_mm", "hT_ready", "qk_mm", "v_mm"))
        part_hi, part_res, part_mid, part_lo, v_ready = (
            sem(n) for n in ("part_hi", "part_res", "part_mid", "part_lo", "v_ready"))
        parts_out = [[sem(f"parts_out{i}{half}") for half in range(2)] for i in range(2)]
        stacks_clear, v_staged = sem("stacks_clear"), sem("v_staged")
        staged = [sem(f"staged{i}") for i in range(NG)]
        q_scores, maxed, k_scores, exped, masked = (
            sem(n) for n in ("q_scores", "maxed", "k_scores", "exped", "masked"))
        pv_done, o_copied, oT_mm, o_rec, o_norm = (
            sem(n) for n in ("pv_done", "o_copied", "oT_mm", "o_rec", "o_norm"))
        m_step, mT_mm, mT_copied, m_rows = (sem(n) for n in ("m_step", "mT_mm", "mT_copied", "m_rows"))
        pool_waited, act_waited, dve_waited = sem("pool_waited"), sem("act_waited"), sem("dve_waited")
        gates_folded, y_cont, yT_mm, yT_ready, proj_mm, bias_in, x1_ready = (
            sem(n) for n in ("gates_folded", "y_cont", "yT_mm", "yT_ready", "proj_mm", "bias_in", "x1_ready"))
        n2_stats, n2_aggr, n2_step, rstd2_ready, h2_step, h2_ready, h2_kept, h2T_mm, h2T_ready = (
            sem(n) for n in ("n2_stats", "n2_aggr", "n2_step", "rstd2_ready", "h2_step", "h2_ready", "h2_kept",
                             "h2T_mm", "h2T_ready"))
        logit_mm, logit_ready, route_step, lg_shifted, exp_l, chosen, prefix_mm, prefix_read, idx_ready, scattered = (
            sem(n) for n in ("logit_mm", "logit_ready", "route_step", "lg_shifted", "exp_l", "chosen", "prefix_mm",
                             "prefix_read", "idx_ready", "scattered"))
        last_norm = sem("last_norm")
        iotas, rev_ready, dest_ready, dest_in = (sem(n) for n in ("iotas", "rev_ready", "dest_ready", "dest_in"))
        redo_ready, last_step, redo_step, above_part, above_mm = (
            sem(n) for n in ("redo_ready", "last_step", "redo_step", "above_part", "above_mm"))
        bis_step, bis_part, bis_count, redo_prefix_in, redo_prefix_mm, redo_idx, redo_rows, resent, dispatched = (
            sem(n) for n in ("bis_step", "bis_part", "bis_count", "redo_prefix_in", "redo_prefix_mm", "redo_idx",
                             "redo_rows", "resent", "dispatched"))
        rows_in = [sem(f"rows_in{i}") for i in range(2)]
        weights_in = [sem(f"weights_in{i}") for i in range(2)]
        w_high, w_low, rT_mm, x_high, x_low, dest_kept = (
            sem(n) for n in ("w_high", "w_low", "rT_mm", "x_high", "x_low", "dest_kept"))
        gate_mm = sem("gate_mm")
        up_mm, silu_ready, hid_ready, down_mm, y_ready = (
            sem(n) for n in ("up_mm", "silu_ready", "hid_ready", "down_mm", "y_ready"))
        w2_in = [sem(f"w2_in{i}") for i in range(2)]
        sent = [sem(f"sent{i}") for i in range(2)]
        res_in = [sem(f"res_in{b}") for b in range(NB)]
        scaled, summed, gated, finished = (sem(n) for n in ("scaled", "summed", "gated", "finished"))
        ended = sem("ended")

        block = ctx.enter_context(nc.Block())

        QB = [0, 2]
        KB = [4, 5]
        PV, MISC = 6, 7

        def masks_before(kind):
            return sum(MASKED[:kind])

        @block.sync
        def _(sp):
            sp.dma_start(ct[:], cT).then_inc(wmod_in, 16)
            sp.dma_start(wmod_s[:], wmod).then_inc(wmod_in, 16)
            for c in range(4):
                sp.dma_start(xs[:, 8 * c:8 * c + 8, :],
                             x.rearrange("b (t p) d -> p (b t) d", p=P)[:, 8 * c:8 * c + 8, :]).then_inc(x_in[c], 16)
            sp.dma_start(wqkv_s[:], wqkvT).then_inc(w_in, 16)
            sp.dma_start(bqkv_s[:], bqkv).then_inc(w_in, 16)
            sp.dma_start(bv_row[:], bv.to_broadcast([P, D])).then_inc(w_in, 16)
            sp.dma_start(bo_row[:], bout.to_broadcast([P, D])).then_inc(w_in, 16)
            sp.dma_start(wo_s[:], woT).then_inc(w_in, 16)
            sp.dma_start(rT_s[:], rT).then_inc(w_in, 16)

            sp.wait_ge(fill_ready, 3)
            sp.dma_start(slot_rows.rearrange("(p s) r -> p s r", p=P),
                         fill[:].unsqueeze(1).to_broadcast([P, SLOTS // P, ROW])).then_inc(filled, 16)
            sp.dma_start(results.rearrange("(p s) r -> p s r", p=P),
                         fill[:, 0:D].unsqueeze(1).to_broadcast([P, 2 * T // P, D])).then_inc(filled, 16)
            def parts_to_dram(b):
                for half in range(2):
                    for j, dst in enumerate((q_parts, k_parts)):
                        sp.wait_ge(part_lo, b * 4 + 2 * half + j + 1)
                        for part in range(3):
                            sp.dma_start(dst[bass.ds(b * NG, NG), part, :, 512 * half:512 * half + 512],
                                         parts[b % 2][half][j][:, part, :]).then_inc(parts_out[b % 2][half], 16)

            def stage(n, buf):
                for src, dst, runs in (
                    (q_parts, qst[buf], ((0, 0, 1), (8, 0, 1), (16, 0, 1), (24, 1, 1), (32, 1, 1), (40, 2, 1))),
                    (k_parts, kst[buf], ((0, 0, 3), (24, 0, 2), (40, 0, 1))),
                ):
                    for row, part, k in runs:
                        sp.dma_start(dst[row:row + 8 * k, :, :].rearrange("p h q -> p (h q)"),
                                     src[bass.ds(n, 1), part:part + k, :, :]
                                     .rearrange("n k (d h) q -> (n k d) (h q)", h=GH)).then_inc(staged[buf], 16)

            def m_move(n, buf):
                sp.wait_ge(mT_copied, n + 1)
                for part in range(3):
                    sp.dma_start(qst[buf][96 + part:97 + part, :, :].rearrange("p h (i q) -> p (h i) q", q=P),
                                 mT[32 * part:32 * part + 32, :]).then_inc(m_rows, 16)

            parts_to_dram(0)
            for half in range(2):
                sp.wait_ge(parts_out[0][half], 96)
            sp.wait_ge(stacks_clear, 2 * NG)
            stage(0, 0)
            for b in range(1, NB):
                parts_to_dram(b)
            for n in range(1, NG):
                stage(n, n)
            for i in range(2):
                for half in range(2):
                    sp.wait_ge(parts_out[i][half], 96 * NB // 2)
            m_move(0, 0)

            def load_weights(e, q):
                for i, w in enumerate((w1T, wgT)):
                    sp.dma_start(w_raw[q][:, i * F:(i + 1) * F], w[bass.ds(e, 1), :, :].rearrange("e h f -> (e h) f")
                                 ).then_inc(weights_in[q], 16)

            def load_second_weights(e, q):
                sp.dma_start(w_raw[q][:, 2 * F:3 * F].rearrange("p (c d) -> p c d", c=FC),
                             w2T[bass.ds(e, 1), :, :].rearrange("e (c p) h -> p (e c) h", p=P)
                             ).then_inc(w2_in[q], 16)

            def load_rows(e, q):
                sp.dma_start(xr[q], slot_rows[bass.ds(e * CAP, CAP), :].rearrange("(s p) r -> p s r", p=P)
                             ).then_inc(rows_in[q], 16)

            for q in range(2):
                load_weights(q, q)
                load_second_weights(q, q)

            def group(b, m, more):
                n = b * NG + m
                m_move(n + 1, (m + 1) % NG)
                if more:
                    sp.wait_ge(k_scores, n * NKU + NKU)
                    stage(n + NG, m)

            with sp.Fori(0, NB - 1) as b:
                for m in range(NG):
                    group(b, m, True)
            for m in range(NG - 1):
                group(NB - 1, m, False)
            sp.wait_ge(k_scores, NN * NKU)
            sp.wait_ge(dispatched, 1)
            for q in range(2):
                load_rows(q, q)
            with sp.Fori(0, 3) as j:
                for q in range(2):
                    e = j * 2 + q
                    sp.wait_ge(w_low, e + 1)
                    load_weights(e + 2, q)
                    sp.wait_ge(rT_mm, e * 3 + 3)
                    sp.wait_ge(dest_kept, e + 1)
                    load_rows(e + 2, q)
                    sp.wait_ge(down_mm, e * 3 + 3)
                    load_second_weights(e + 2, q)
            for q in range(2):
                sp.wait_ge(sent[q], 4 * 16 * ST)
            for b in range(NB):
                for k, g in enumerate((g1, g2)):
                    sp.dma_start(g[:, b * BT:b * BT + BT, :],
                                 results[k * T + b * S:k * T + b * S + S, :].rearrange("(t p) d -> p t d", p=P)
                                 ).then_inc(res_in[b], 16)
            for b in range(NB):
                sp.wait_ge(finished, b + 1)
                sp.dma_start(out[b].rearrange("(t p) d -> p t d", p=P), g1[:, b * BT:b * BT + BT, :]
                             ).then_inc(ended, 16)
            sp.wait_ge(ended, 16 * NB)

        @block.gpsimd
        def _(pool):
            nc.gpsimd.memset(fill[:], 0.0).then_inc(fill_ready, 1)
            pool.wait_ge(fill_ready, 1)
            nc.gpsimd.memset(fill[:, D:ROW].bitcast(I32), int(FAR)).then_inc(fill_ready, 2)
            nc.gpsimd.memset(mhalf[:], -0.5).then_inc(consts_ready, 1)
            for m in (identf, identb):
                nc.gpsimd.memset(m[:], 0.0).then_inc(consts_ready, 1)
            nc.gpsimd.memset(cmask[:], 0.0).then_inc(consts_ready, 1)
            nc.gpsimd.memset(before[:], 1.0).then_inc(consts_ready, 1)
            nc.gpsimd.memset(onesb[:], 1.0).then_inc(consts_ready, 1)
            pool.wait_ge(consts_ready, 6)
            for m in (identf, identb):
                nc.gpsimd.affine_select(out=m[:], in_=m[:], compare_op=ALU.not_equal, fill=1.0, base=0,
                                        pattern=[[-1, P]], channel_multiplier=1).then_inc(consts_ready, 1)
            nc.gpsimd.affine_select(out=cmask[:], in_=cmask[:], compare_op=ALU.is_ge, fill=NEG, base=0,
                                    pattern=[[-1, P]], channel_multiplier=1).then_inc(consts_ready, 1)
            nc.gpsimd.affine_select(out=before[:], in_=before[:], compare_op=ALU.is_gt, fill=0.0, base=0,
                                    pattern=[[1, P]], channel_multiplier=-1).then_inc(consts_ready, 1)
            for i in range(2):
                nc.gpsimd.memset(stack[:, 2048 * (NG + i):2048 * (NG + i) + 2048], 0.0).then_inc(stacks_clear, 1)
            def deviation(b):
                pool.wait_ge(ln_eps, b + 1)
                nc.gpsimd.tensor_tensor(rstd[:], vpe[:], mhalf[:], ALU.pow).then_inc(ln_rstd, 1)

            deviation(0)
            for i in range(2, NG):
                nc.gpsimd.memset(stack[:, 2048 * (NG + i):2048 * (NG + i) + 2048], 0.0).then_inc(stacks_clear, 1)
            deviation(1)
            for i in range(2):
                nc.gpsimd.memset(vst[i][:], 0.0).then_inc(v_staged, 1)

            def low_parts(b):
                for half in range(2):
                    for j in range(2):
                        pool.wait_ge(part_mid, b * 4 + 2 * half + j + 1)
                        pool.sem_inc(pool_waited, 1)
                        nc.gpsimd.tensor_tensor(parts[b % 2][half][j][:, 2, :], pres[half][j], parts[b % 2][half][j][:, 1, :],
                                                ALU.subtract).then_inc(part_lo, 1)

            low_parts(0)
            for b in range(1, NB - 1):
                deviation(b + 1)
                low_parts(b)
            low_parts(NB - 1)
            pool.wait_ge(stacks_clear, 2 * NG)
            pool.wait_ge(v_staged, 2)
            pool.wait_ge(part_lo, 4 * NB)
            for i in range(NG):
                nc.gpsimd.memset(stack[96:99, 2048 * (NG + i):2048 * (NG + i) + 2048].bitcast(I32), 0x3F803F80
                                 ).then_inc(stacks_clear, 1)
                pool.wait_ge(stacks_clear, 2 * NG + 1 + i)
            for i in range(2):
                nc.gpsimd.memset(vst[i][:, :, :, HD:HD + 1], 1.0).then_inc(v_staged, 1)
            nc.gpsimd.iota(rev_i[:, 0, :], pattern=[[-1, NE]], base=NE, channel_multiplier=0).then_inc(iotas, 1)
            nc.gpsimd.iota(rev_i[:, 1, :], pattern=[[CAP, NE]], base=0, channel_multiplier=0).then_inc(iotas, 1)
            nc.gpsimd.memset(onesf[:], 1.0).then_inc(iotas, 1)
            nc.gpsimd.memset(used[:], 0.0).then_inc(iotas, 1)
            nc.gpsimd.memset(small[:], 1.0).then_inc(iotas, 1)
            nc.gpsimd.iota(dests[:], pattern=[[T, 2], [P, NT]], base=0, channel_multiplier=1).then_inc(dest_ready, 1)

            def stage_v(n, buf):
                nc.gpsimd.tensor_copy(
                    vst[buf][:, :, :, 0:HD],
                    vals[:, bass.ds(n, 1), :, :].rearrange("p n t (h d) -> p (n t) h d", h=GH)
                ).then_inc(v_staged, 1)

            pool.wait_ge(v_ready, 2 * NB)
            pool.wait_ge(v_staged, 4)
            stage_v(0, 0)
            pool.wait_ge(gates_ready, 6)
            pool.wait_ge(w_in, 96)
            for b in range(NB):
                nc.gpsimd.tensor_tensor(wog[:, b, :], wo_s[:], modrow[:, b, 0, :], ALU.mult).then_inc(gates_folded, 1)
                nc.gpsimd.tensor_tensor(gab[:, b, :], bo_row[:], modrow[:, b, 0, :], ALU.mult
                                        ).then_inc(gates_folded, 1)
            pool.wait_ge(gates_folded, 2 * NB)
            pool.wait_ge(dest_ready, 1)
            pool.wait_ge(filled, 32)

            def gather_heads(b):
                pool.wait_ge(o_norm, b * (2 * NG) + 2 * NG)
                pool.sem_inc(pool_waited, 1)
                for half in range(2):
                    nc.gpsimd.tensor_copy(
                        yc[half][:].rearrange("p t (g d) -> p t g d", g=NG),
                        ys[:, bass.ds(b * NG, NG), 4 * half:4 * half + 4, :].rearrange("p g t d -> p t g d")
                    ).then_inc(y_cont, 1)
                for half in range(2):
                    xv = xs[:, bass.ds(b * BT + 4 * half, 4), :]
                    nc.gpsimd.tensor_tensor(xv, xv, gab[:, bass.ds(b, 1), :].to_broadcast([P, 4, D]),
                                            ALU.add).then_inc(bias_in, 1)

            def second_deviation(b, half):
                pool.wait_ge(n2_step, b * 2 + half + 1)
                nc.gpsimd.tensor_tensor(rstd2[half][:], vpe2[half][:], mhalf[:, 0:4], ALU.pow
                                        ).then_inc(rstd2_ready, 1)

            def second_norm(b, half):
                c = b * 2 + half
                second_deviation(b, half)
                h = rows[:, 0, 4 * half:4 * half + 4, 0:D]
                nc.gpsimd.tensor_tensor(h, xs[:, bass.ds(c * 4, 4), :],
                                        mv2[half][:, :, 0:1].to_broadcast([P, 4, D]), ALU.subtract
                                        ).then_inc(h2_step, 1)
                pool.wait_ge(rstd2_ready, c + 1)
                pool.wait_ge(h2_step, c * 3 + 1)
                nc.gpsimd.tensor_tensor(h, h, rstd2[half][:].unsqueeze(2).to_broadcast([P, 4, D]), ALU.mult
                                        ).then_inc(h2_step, 1)
                pool.wait_ge(h2_step, c * 3 + 2)
                pool.sem_inc(pool_waited, 1)
                nc.gpsimd.tensor_tensor(h, h, modrow[:, bass.ds(b, 1), 2, :].to_broadcast([P, 4, D]), ALU.mult
                                        ).then_inc(h2_step, 1)
                pool.wait_ge(h2_step, c * 3 + 3)
                pool.sem_inc(pool_waited, 1)
                nc.gpsimd.tensor_tensor(h, h, modrow[:, bass.ds(b, 1), 1, :].to_broadcast([P, 4, D]), ALU.add
                                        ).then_inc(h2_ready, 1)

            def keep_rows(b, half):
                c = b * 2 + half
                h = rows[:, 0, 4 * half:4 * half + 4, 0:D]
                pool.wait_ge(h2_ready, c + 1)
                pool.sem_inc(pool_waited, 1)
                nc.gpsimd.tensor_copy(rows[:, 1, 4 * half:4 * half + 4, 0:D], h).then_inc(h2_kept, 1)
                nc.gpsimd.tensor_copy(kept_rows[:, bass.ds(c * 4, 4), :], h).then_inc(h2_kept, 1)

            def row_dests(b):
                nc.gpsimd.tensor_copy(rows[:, :, :, D:ROW].bitcast(I32).rearrange("p k t r -> p k (t r)"),
                                      dests[:, :, bass.ds(b * BT, BT)]).then_inc(dest_in, 1)

            def scatter(b):
                pool.wait_ge(idx_ready, b * 2 + 2)
                pool.wait_ge(h2_kept, b * 4 + 4)
                pool.wait_ge(dest_in, b + 1)
                pool.sem_inc(pool_waited, 1)
                for t in range(BT):
                    for k in range(2):
                        nc.gpsimd.indirect_dma_start(
                            slot_rows, bass.IndirectOffsetOnAxis(ap=idxb[:, k, t:t + 1], axis=0),
                            rows[:, k, t, :], None, bounds_check=SLOTS - 1, oob_is_err=False).then_inc(scattered, 16)

            def group(b, m, last, mix):
                n = b * NG + m
                for kind in range(NK):
                    if MASKED[kind]:
                        pool.wait_ge(exped, n * NKU + GH * kind + GH)
                        pool.sem_inc(pool_waited, 1)
                        done = [p for p in KUNITS[kind] if diagonal(p)]
                        for piece in done:
                            col = piece[4]
                            v = probs[kind % NP][:, :, col:col + P]
                            ins = nc.gpsimd.affine_select(out=v, in_=v, compare_op=ALU.is_ge, fill=0.0, base=0,
                                                          pattern=[[0, GH], [1, P]], channel_multiplier=-1)
                        ins.then_inc(masked, 1)
                    if kind == 2:
                        if not last:
                            after(pool, pv_done, n * NK)
                            pool.sem_inc(pool_waited, 1)
                            stage_v(n + 1, (m + 1) % 2)
                        if mix and m == 0:
                            gather_heads(b - 1)
                        if mix and m == 1:
                            for half in range(2):
                                second_norm(b - 1, half)
                        if mix and m == 2:
                            row_dests(b - 1)
                            for half in range(2):
                                keep_rows(b - 1, half)
                        if mix and m == 3:
                            scatter(b - 1)
                if mix and m == 3:
                    pool.wait_ge(scattered, b * (32 * BT))

            for m in range(NG):
                group(0, m, False, False)
            with pool.Fori(1, NB - 1) as b:
                for m in range(NG):
                    group(b, m, False, True)
            for m in range(NG):
                group(NB - 1, m, m == NG - 1, True)
            b = NB - 1
            for half in range(2):
                xv = xs[:, b * BT + 4 * half:b * BT + 4 * half + 4, :]
                nc.gpsimd.tensor_tensor(xv, xv, gab[:, b:b + 1, :].to_broadcast([P, 4, D]), ALU.add).then_inc(bias_in, 1)
            for half in range(2):
                pool.wait_ge(o_norm, 2 * NN - 1 + half)
                nc.gpsimd.tensor_copy(
                    yc[half][:].rearrange("p t (g d) -> p t g d", g=NG),
                    ys[:, b * NG:b * NG + NG, 4 * half:4 * half + 4, :].rearrange("p g t d -> p t g d")
                ).then_inc(y_cont, 1)
            row_dests(NB - 1)
            for half in range(2):
                second_deviation(NB - 1, half)
            for half in range(2):
                keep_rows(NB - 1, half)

            def low_weights(e, q):
                pool.wait_ge(w_high, e + 1)
                pool.sem_inc(pool_waited, 1)
                nc.gpsimd.tensor_tensor(w_l[q][:], w_raw[q][:, 0:2 * F], w_h[q][:].bitcast(F32), ALU.subtract).then_inc(w_low, 1)

            for q in range(2):
                low_weights(q, q)
            scatter(NB - 1)
            pool.wait_ge(redo_ready, 1)
            again = pool.value_load(redo[0:1, 0:1], min_val=0, max_val=1)
            pool.wait_ge(scattered, NB * 32 * BT)
            with pool.If(again > 0):
                pool.wait_ge(redo_idx, 2)
                for b in range(NB):
                    for k in range(2):
                        nc.gpsimd.tensor_copy(rows[:, k, :, 0:D], kept_rows[:, b * BT:b * BT + BT, :]
                                              ).then_inc(redo_rows, 1)
                    nc.gpsimd.tensor_copy(rows[:, :, :, D:ROW].bitcast(I32).rearrange("p k t r -> p k (t r)"),
                                          dests[:, :, b * BT:b * BT + BT]).then_inc(redo_rows, 1)
                    pool.wait_ge(redo_rows, 3 * b + 3)
                    for t in range(BT):
                        for k in range(2):
                            nc.gpsimd.indirect_dma_start(
                                slot_rows, bass.IndirectOffsetOnAxis(ap=idx[:, k, b * BT + t:b * BT + t + 1], axis=0),
                                rows[:, k, t, :], None, bounds_check=SLOTS - 1, oob_is_err=False
                            ).then_inc(resent, 16)
                    pool.wait_ge(resent, (b + 1) * 32 * BT)
            pool.sem_inc(dispatched, 1)

            def send(e, q):
                for n, (s0, ns) in enumerate(CH):
                    pool.wait_ge(y_ready, e * 3 + n + 1)
                    pool.sem_inc(pool_waited, 1)
                    for st in range(s0, s0 + ns):
                        nc.gpsimd.indirect_dma_start(
                            results, bass.IndirectOffsetOnAxis(ap=dest_of[q][:, st:st + 1], axis=0),
                            yo[q][:, st, :], None, bounds_check=2 * T - 1, oob_is_err=False).then_inc(sent[q], 16)

            with pool.Fori(0, NE // 2 - 1) as j:
                for q in range(2):
                    send(j * 2 + q, q)
                    low_weights(j * 2 + q + 2, q)
            for q in range(2):
                send(NE - 2 + q, q)

            for b in range(NB):
                pool.wait_ge(gated, b + 1)
                v = g1[:, b * BT:b * BT + BT, :]
                nc.gpsimd.tensor_tensor(v, v, xs[:, b * BT:b * BT + BT, :], ALU.add).then_inc(finished, 1)

        @block.tensor
        def _(pe):
            pe.wait_ge(wmod_in, 32)
            pe.wait_ge(silu_c, 1)
            for j in range(2):
                mm = nc.tensor.matmul(psum[:, MISC, j * NB:j * NB + NB], wmod_s[:, j * D:j * D + D], sc[:],
                                      start=True, stop=True)
            mm.then_inc(modcol_mm, 1)
            pe.wait_ge(wide_c, 1)
            for b in range(NB):
                nc.tensor.matmul(psum[:, b, :], scb[:, b, :], wmod_s[:, 2 * D:6 * D],
                                 start=True, stop=True).then_inc(modrow_mm, 1)
            pe.wait_ge(consts_ready, 10)
            pe.wait_ge(w_in, 96)
            pe.wait_ge(modrow_copied, 2 * NB)

            def turn_normed(b, half):
                pe.wait_ge(ln_norm, b * 2 + half + 1)
                for i in range(4):
                    mm = nc.tensor.transpose(psum[:, half, i * P:i * P + P], xn[half][:, i, :], identf[:])
                mm.then_inc(xT_mm, 1)

            def project(b, half):
                pe.wait_ge(hT_ready, b * 2 + half + 1)
                after(pe, part_res, b * 4 + 2 * half - 2)
                after(pe, v_ready, b * 2 + half - 1)
                for j in range(2):
                    nc.tensor.matmul(psum[:, 2 + 2 * j + half, :], wqkv_s[:, j * D:j * D + D], hT[half][:],
                                     start=True, stop=True).then_inc(qk_mm, 1)
                for i in range(4):
                    mm = nc.tensor.matmul(psum[:, 6 + half, i * P:i * P + P], hT[half][:, i * P:i * P + P],
                                          wqkv_s[:, 2 * D:3 * D], start=True, stop=True)
                mm.then_inc(v_mm, 1)

            for half in range(2):
                turn_normed(0, half)
            for half in range(2):
                project(0, half)
                turn_normed(1, half)
            with pe.Fori(1, NB - 1) as b:
                for half in range(2):
                    project(b, half)
                    turn_normed(b + 1, half)
            for half in range(2):
                project(NB - 1, half)

            def query_unit(n, buf, u, fresh):
                if not fresh:
                    pe.wait_ge(maxed, n * NQU + u - 1)
                hp, kind = divmod(u, len(QUNITS))
                for e in range(2):
                    h = 2 * hp + e
                    for i, k0, w, col, _ in QUNITS[kind]:
                        diag = k0 + w == (i + 1) * P
                        o = psum[:, QB[u % 2] + e, :]
                        mm = nc.tensor.matmul(o[:, col:col + w], qst[buf][0:96, h, i * P:i * P + P],
                                              kst[buf][0:96, h, k0:k0 + w], start=True, stop=not diag)
                        if diag:
                            mm = nc.tensor.matmul(o[:, col + w - P:col + w], identb[:], cmask[:],
                                                  start=False, stop=True)
                mm.then_inc(q_scores, 1)

            def max_rows(n):
                pe.wait_ge(m_step, (n + 1) * 5)
                nc.tensor.transpose(psum[:, MISC, :].bitcast(BF16)[0:96, 0:P],
                                    mparts[:].rearrange("p a h i -> p (a h i)"), identb[:]).then_inc(mT_mm, 1)

            def key_unit(n, buf, s, fresh):
                if not fresh:
                    pe.wait_ge(exped, n * NKU + s - 1)
                kind, h = divmod(s, GH)
                for kb, qc, q0, w, col in KUNITS[kind]:
                    mm = nc.tensor.matmul(psum[:, KB[s % 2], col:col + w], kst[buf][:, h, kb * P:kb * P + P],
                                          qst[buf][:, h, qc * 512 + q0:qc * 512 + q0 + w], start=True, stop=True)
                mm.then_inc(k_scores, 1)

            def values(n, buf, kind):
                if MASKED[kind]:
                    pe.wait_ge(masked, n * NMASK + masks_before(kind) + 1)
                else:
                    pe.wait_ge(exped, n * NKU + GH * kind + GH)
                pieces = [(kind, p) for p in KUNITS[kind] if not (kind == 2 and p[1] == 1)]
                if kind == 3:
                    pieces += [(2, KUNITS[2][1])]
                for k, (kb, qc, q0, w, col) in pieces:
                    for h in range(GH):
                        mm = nc.tensor.matmul(psum[32 * h:32 * h + 32, PV, q0:q0 + w], vst[buf][:, kb, h, :],
                                              probs[k % NP][:, h, col:col + w],
                                              start=kind in (0, 3) and k == kind, stop=False, skip_group_check=True)
                mm.then_inc(pv_done, 1)

            def turn(count, chunk):
                pe.wait_ge(o_copied, count)
                for i in range(4):
                    mm = nc.tensor.transpose(psum[:, MISC, i * P:i * P + P], osb[chunk][:, i * P:i * P + P], identf[:])
                mm.then_inc(oT_mm, 1)

            def turn_y(b, half, bank):
                pe.wait_ge(y_cont, b * 2 + half + 1)
                for i in range(4):
                    mm = nc.tensor.transpose(psum[:, bank, i * P:i * P + P], yc[half][:, i, :], identf[:])
                mm.then_inc(yT_mm, 1)

            def project_out(b, half, bank):
                pe.wait_ge(yT_ready, b * 2 + half + 1)
                for i in range(4):
                    mm = nc.tensor.matmul(psum[:, bank, i * P:i * P + P], yT[half][:, i * P:i * P + P],
                                          wog[:, bass.ds(b, 1), :].rearrange("p b d -> p (b d)"),
                                          start=True, stop=True)
                mm.then_inc(proj_mm, 1)

            def turn_h2(b, half, bank):
                pe.wait_ge(h2_ready, b * 2 + half + 1)
                for i in range(4):
                    mm = nc.tensor.transpose(psum[:, bank, i * P:i * P + P], rows[:, 0, 4 * half + i, 0:D], identf[:])
                mm.then_inc(h2T_mm, 1)

            def route_logits(b, bank):
                pe.wait_ge(h2T_ready, b * 2 + 2)
                for t in range(BT):
                    half, i = divmod(t, 4)
                    mm = nc.tensor.matmul(psum[:, bank, t * NE:t * NE + NE], h2T[half][:, i * P:i * P + P],
                                          rT_s[:], start=True, stop=True)
                mm.then_inc(logit_mm, 1)

            def prefix_counts(b, bank):
                pe.wait_ge(chosen, b + 1)
                m = maskbb[:].rearrange("p e t -> p (e t)")
                nc.tensor.matmul(psum[:, bank, 0:64], before[:], m, start=True, stop=True)
                nc.tensor.matmul(psum[:, bank, 64:128], onesb[:], m, start=True, stop=True).then_inc(prefix_mm, 1)

            def group(b, m, first, more, mix):
                n = b * NG + m
                nxt = (m + 1) % NG
                p = b - 1
                pe.wait_ge(m_rows, n * 48 + 48)
                pe.wait_ge(v_staged, n + 5)
                for s in range(NKU):
                    key_unit(n, m, s, first and s < 2)
                    for u in range(NQU):
                        if QSTEP[u] == s and more > 0:
                            query_unit(n + 1, nxt, u, False)
                        if QSTEP[u] == s - NKU and more > 1:
                            if u == 0:
                                pe.wait_ge(staged[(m + 2) % NG], (b + (m + 2) // NG) * 144 + 144)
                            query_unit(n + 2, (m + 2) % NG, u, False)
                    if mix and s == 2 and m == 1:
                        pe.wait_ge(mT_copied, n + 1)
                        project_out(p, 0, MISC)
                    if mix and s == 2 and m == 2:
                        pe.wait_ge(mT_copied, n + 1)
                        turn_h2(p, 1, MISC)
                    if s == 3 and not first:
                        values(n - 1, (m + 1) % 2, 8)
                    if mix and s == 5 and m == 3:
                        pe.wait_ge(mT_copied, n + 1)
                        prefix_counts(p, MISC)
                    if s == 9 and not first:
                        if not mix or m == 0:
                            pe.wait_ge(mT_copied, n + 1)
                        elif m == 1:
                            pe.wait_ge(x1_ready, p * 2 + 1)
                        elif m == 2:
                            pe.wait_ge(h2T_ready, p * 2 + 2)
                        else:
                            pe.wait_ge(prefix_read, p + 1)
                        turn(2 * n, 1)
                    if s % 4 == 3 and s >= 7:
                        kind = s // 4 - 1
                        if kind == 0:
                            after(pe, o_copied, 2 * n)
                        if kind == 3:
                            pe.wait_ge(o_copied, 2 * n + 1)
                        values(n, m % 2, kind)
                    if mix and s == 17 and m == 0:
                        pe.wait_ge(o_norm, 2 * n)
                        turn_y(p, 0, MISC)
                    if mix and s == 14 and m == 1:
                        pe.wait_ge(o_norm, 2 * n)
                        project_out(p, 1, MISC)
                    if mix and s == 14 and m == 2:
                        pe.wait_ge(o_norm, 2 * n)
                        route_logits(p, MISC)
                    if s == 22:
                        if mix and m == 0:
                            pe.wait_ge(yT_ready, p * 2 + 1)
                        elif mix and m == 1:
                            pe.wait_ge(x1_ready, p * 2 + 2)
                        elif mix and m == 2:
                            pe.wait_ge(logit_ready, p + 1)
                        else:
                            after(pe, o_norm, 2 * n)
                        turn(2 * n + 1, 0)
                    if mix and s == 26 and m == 0:
                        pe.wait_ge(o_norm, 2 * n + 1)
                        turn_y(p, 1, MISC)
                    if mix and s == 26 and m == 1:
                        pe.wait_ge(o_norm, 2 * n + 1)
                        turn_h2(p, 0, MISC)
                    if s == MSTEP and more > 0:
                        if mix and m == 0:
                            pe.wait_ge(yT_ready, p * 2 + 2)
                        elif mix and m == 1:
                            pe.wait_ge(h2T_ready, p * 2 + 1)
                        else:
                            pe.wait_ge(o_norm, 2 * n + 1)
                        max_rows(n + 1)

            pe.wait_ge(part_res, 4 * NB)
            pe.wait_ge(v_ready, 2 * NB)
            pe.wait_ge(staged[0], 144)
            pe.wait_ge(stacks_clear, 2 * NG)
            for u in range(NQU):
                query_unit(0, 0, u, u < 2)
            max_rows(0)
            pe.wait_ge(staged[1], 144)
            for u in range(EARLY):
                query_unit(1, 1, u, False)
            pe.wait_ge(stacks_clear, 3 * NG)
            for m in range(NG):
                group(0, m, m == 0, 2, False)
            with pe.Fori(1, NB - 1) as b:
                for m in range(NG):
                    group(b, m, False, 2, True)
            for m in range(NG):
                group(NB - 1, m, False, min(2, NG - 1 - m), True)
            values(NN - 1, (NN - 1) % 2, 8)
            pe.wait_ge(o_norm, 2 * NN - 1)
            turn(2 * NN, 1)

            pe.wait_ge(o_norm, 2 * NN)
            pe.wait_ge(exped, NN * NKU)
            for half in range(2):
                turn_y(NB - 1, half, half)
            for half in range(2):
                project_out(NB - 1, half, 2 + half)
            for half in range(2):
                turn_h2(NB - 1, half, 4 + half)
            route_logits(NB - 1, PV)
            prefix_counts(NB - 1, MISC)

            pe.wait_ge(redo_ready, 1)
            again = pe.value_load(redo[0:1, 0:1], min_val=0, max_val=1)
            with pe.If(again > 0):
                with pe.Fori(0, 30) as i:
                    pe.wait_ge(bis_part, i + 1)
                    nc.tensor.matmul(psum[:, 0, 0:NE], onesb[:], part8[:], start=True, stop=True).then_inc(bis_count, 1)
                pe.wait_ge(above_part, 1)
                nc.tensor.matmul(psum[:, 3, 0:NE], onesb[:], part8[:], start=True, stop=True).then_inc(above_mm, 1)
                for k in range(2):
                    pe.wait_ge(redo_prefix_in, k + 1)
                    m = maskb[:].rearrange("p e t -> p (e t)")
                    nc.tensor.matmul(psum[:, 1 + k, 0:256], before[:], m, start=True, stop=True)
                    nc.tensor.matmul(psum[:, 1 + k, 256:512], onesb[:], m, start=True, stop=True
                                     ).then_inc(redo_prefix_mm, 1)

            def turn_rows(e, q, n):
                s0, ns = CH[n]
                if n < 2:
                    after(pe, x_low, e * 3 if n == 0 else e * 3 - 1)
                else:
                    pe.wait_ge(x_low, e * 3 + 1)
                for i in range(ns):
                    mm = nc.tensor.transpose(psum[:, n % 2, i * P:i * P + P], xr[q][:, s0 + i, 0:D], identf[:])
                mm.then_inc(rT_mm, 1)

            def split_product(out_ap, left, right):
                for i, (a, b) in enumerate(((0, 0), (0, 1), (1, 0))):
                    mm = nc.tensor.matmul(out_ap, left[a], right[b], start=i == 0, stop=i == 2)
                return mm

            def up(e, q, n):
                s0, ns = CH[n]
                for f in range(FC):
                    k = (e * 3 + n) * FC + f
                    for j, read, done in ((1, silu_ready, gate_mm), (0, hid_ready, up_mm)):
                        after(pe, read, k - 1)
                        c = j * F + f * P
                        mm = split_product(psum[:, 2 + 2 * (f % 2) + j, 0:ns * P],
                                           (w_h[q][:, c:c + P], w_l[q][:, c:c + P]),
                                           tuple(x[q][:, s0 * P:(s0 + ns) * P] for x in (x_h, x_l)))
                        mm.then_inc(done, 1)

            def down(e, q, n, par):
                s0, ns = CH[n]
                pe.wait_ge(hid_ready, (e * 3 + n) * FC + FC)
                after(pe, y_ready, e * 3 + n - 1)
                for i in range(ns):
                    for f in range(FC):
                        c = 2 * F + f * D
                        mm = nc.tensor.matmul(psum[:, 6 + par, i * P:i * P + P], hid[par][:, f, i * P:i * P + P],
                                              w_raw[q][:, c:c + D], start=f == 0, stop=f == FC - 1)
                mm.then_inc(down_mm, 1)

            def expert(j, q, last):
                e = j * 2 + q
                pe.wait_ge(w_low, e + 1)
                pe.wait_ge(x_low, e * 3 + 3)
                up(e, q, 0)
                up(e, q, 1)
                pe.wait_ge(w2_in[q], j * 16 + 16)
                down(e, q, 0, q)
                up(e, q, 2)
                if not last:
                    pe.wait_ge(rows_in[1 - q], (j + q) * 16 + 16)
                    turn_rows(e + 1, 1 - q, 0)
                    turn_rows(e + 1, 1 - q, 1)
                down(e, q, 1, 1 - q)
                if not last:
                    turn_rows(e + 1, 1 - q, 2)
                down(e, q, 2, q)

            pe.wait_ge(rows_in[0], 16)
            for n in range(3):
                turn_rows(0, 0, n)
            for q in range(2):
                expert(0, q, False)
            with pe.Fori(1, NE // 2 - 1) as j:
                for q in range(2):
                    expert(j, q, False)
            for q in range(2):
                expert(NE // 2 - 1, q, q == 1)

        @block.scalar
        def _(act):
            act.wait_ge(wmod_in, 32)
            nc.scalar.activation(et[:], ct[:], ACT.Exp, scale=-1.0).then_inc(exp_c, 1)
            for i in range(NG // 2):
                nc.scalar.memzero(stack[:, 2048 * i:2048 * i + 2048]).then_inc(stacks_clear, 1)
            for b in range(NB):
                act.wait_ge(modrow_mm, b + 1)
                nc.scalar.activation(modrow[:, b, 0:2, :], psum[:, b, 0:256], ACT.Copy).then_inc(modrow_copied, 1)
                nc.scalar.activation(modrow[:, b, 2:4, :], psum[:, b, 256:512], ACT.Copy).then_inc(modrow_copied, 1)

            act.wait_ge(modcol_ready, 2)

            def modulate(b, half):
                act.wait_ge(xT_mm, b * 2 + half + 1)
                act.sem_inc(act_waited, 1)
                nc.scalar.activation(hT[half][:], psum[:, half, :], ACT.Identity,
                                     bias=modcol[:, 0, bass.ds(b, 1)], scale=modcol[:, 1, bass.ds(b, 1)]
                                     ).then_inc(hT_ready, 1)

            def high_parts(b, half):
                c = b * 2 + half
                for j in range(2):
                    act.wait_ge(qk_mm, c * 2 + j + 1)
                    if j == 0 and b >= 2:
                        act.wait_ge(parts_out[b % 2][half], b // 2 * 96)
                    nc.scalar.activation(parts[b % 2][half][j][:, 0, :], psum[:, 2 + 2 * j + half, :], ACT.Identity,
                                         bias=bqkv_s[:, j:j + 1]).then_inc(part_hi, 1)

            def middle_parts(b, half):
                for j in range(2):
                    act.wait_ge(part_res, b * 4 + 2 * half + j + 1)
                    nc.scalar.activation(parts[b % 2][half][j][:, 1, :], pres[half][j], ACT.Copy).then_inc(part_mid, 1)

            for half in range(2):
                modulate(0, half)
            for i in range(NG // 2, NG):
                nc.scalar.memzero(stack[:, 2048 * i:2048 * i + 2048]).then_inc(stacks_clear, 1)
            for b in range(NB - 1):
                for half in range(2):
                    high_parts(b, half)
                    modulate(b + 1, half)
                    middle_parts(b, half)
            for half in range(2):
                high_parts(NB - 1, half)
                middle_parts(NB - 1, half)

            def max_copy(n):
                act.wait_ge(mT_mm, n + 1)
                if not (isinstance(n, int) and n == 0):
                    act.wait_ge(m_rows, n * 48)
                nc.scalar.activation(mT[:], psum[:, MISC, :].bitcast(BF16)[0:96, 0:P], ACT.Copy
                                     ).then_inc(mT_copied, 1)

            def out_copy(count, chunk, turned):
                act.wait_ge(pv_done, count)
                after(act, oT_mm, turned)
                nc.scalar.activation(osb[chunk][:], psum[:, PV, :], ACT.Copy).then_inc(o_copied, 1)

            def y_out(b, half, bank):
                act.wait_ge(yT_mm, b * 2 + half + 1)
                nc.scalar.activation(yT[half][:], psum[:, bank, :], ACT.Copy).then_inc(yT_ready, 1)

            def h2_out(b, half, bank):
                act.wait_ge(h2T_mm, b * 2 + half + 1)
                nc.scalar.activation(h2T[half], psum[:, bank, :], ACT.Copy).then_inc(h2T_ready, 1)

            def logits_exp(b):
                act.wait_ge(lg_shifted, b + 1)
                act.sem_inc(act_waited, 1)
                nc.scalar.activation(lg[:], lg[:], ACT.Exp).then_inc(exp_l, 1)

            def group(b, m, first, last, mix):
                n = b * NG + m
                for s in range(NKU):
                    kind, h = divmod(s, GH)
                    if h == 0:
                        if kind >= NP:
                            act.wait_ge(pv_done, n * NK + (4 if kind == 5 else kind - 2))
                        elif not first:
                            act.wait_ge(pv_done, n * NK + kind - 2)
                    act.wait_ge(k_scores, n * NKU + s + 1)
                    nc.scalar.activation(probs[kind % NP][:, h, :], psum[:, KB[s % 2], :], ACT.Exp,
                                         scale=SCALE).then_inc(exped, 1)
                    if s == 5 and not first:
                        out_copy(n * NK, 1, n * 2 - 2)
                    if s == 17:
                        out_copy(n * NK + 3, 0, n * 2 - 1)
                    if mix and m == 0 and s in (18, 27):
                        y_out(b - 1, s // 27, MISC)
                    if mix and m == 1 and s == 27:
                        h2_out(b - 1, 0, MISC)
                    if mix and m == 2 and s == 3:
                        h2_out(b - 1, 1, MISC)
                    if mix and m == 2 and s == 20:
                        logits_exp(b - 1)
                    if s == MSTEP and not last:
                        max_copy(n + 1)

            max_copy(0)
            for m in range(NG):
                group(0, m, m == 0, False, False)
            with act.Fori(1, NB - 1) as b:
                for m in range(NG):
                    group(b, m, False, False, True)
            for m in range(NG):
                group(NB - 1, m, False, m == NG - 1, True)
            out_copy(NN * NK, 1, NN * 2 - 2)

            for half in range(2):
                y_out(NB - 1, half, half)

            def high_weights(e, q, k):
                act.wait_ge(weights_in[q], k * 32 + 32)
                act.sem_inc(act_waited, 1)
                nc.scalar.activation(w_h[q][:], w_raw[q][:, 0:2 * F], ACT.Copy).then_inc(w_high, 1)

            for q in range(2):
                high_weights(q, q, 0)
            for half in range(2):
                h2_out(NB - 1, half, 4 + half)
            logits_exp(NB - 1)

            def high_rows(e, q, n):
                s0, ns = CH[n]
                act.wait_ge(rT_mm, e * 3 + n + 1)
                nc.scalar.activation(x_h[q][:, s0 * P:(s0 + ns) * P], psum[:, n % 2, 0:ns * P], ACT.Copy
                                     ).then_inc(x_high, 1)

            def silu(e, n):
                ns = CH[n][1]
                for f in range(FC):
                    k = (e * 3 + n) * FC + f
                    after(act, hid_ready, k - 1)
                    act.wait_ge(gate_mm, k + 1)
                    nc.scalar.activation(sg[f % 2][:, 0:ns * P], psum[:, 3 + 2 * (f % 2), 0:ns * P], ACT.Silu
                                         ).then_inc(silu_ready, 1)

            def results_out(e, q, n, par):
                s0, ns = CH[n]
                act.wait_ge(down_mm, e * 3 + n + 1)
                nc.scalar.activation(yo[q][:, s0:s0 + ns, :],
                                     psum[:, 6 + par, 0:ns * P].rearrange("p (s d) -> p s d", s=ns), ACT.Copy
                                     ).then_inc(y_ready, 1)

            def expert(j, q, last):
                e = j * 2 + q
                silu(e, 0)
                silu(e, 1)
                after(act, sent[q], j * (16 * ST))
                results_out(e, q, 0, q)
                silu(e, 2)
                if not last:
                    high_rows(e + 1, 1 - q, 0)
                    high_rows(e + 1, 1 - q, 1)
                results_out(e, q, 1, 1 - q)
                if not last:
                    high_rows(e + 1, 1 - q, 2)
                results_out(e, q, 2, q)
                if not (isinstance(j, int) and j == NE // 2 - 1):
                    high_weights(e + 2, q, j + 1)

            for n in range(3):
                high_rows(0, 0, n)
            for q in range(2):
                expert(0, q, False)
            with act.Fori(1, NE // 2 - 1) as j:
                for q in range(2):
                    expert(j, q, False)
            for q in range(2):
                expert(NE // 2 - 1, q, q == 1)

            for t in range(NT):
                if t % BT == 0:
                    act.wait_ge(res_in[t // BT], 32)
                nc.scalar.activation(g1[:, t, :], g1[:, t, :], ACT.Copy, scale=kw1[:, t:t + 1]).then_inc(scaled, 1)

        @block.vector
        def _(dve):
            dve.wait_ge(exp_c, 1)
            nc.vector.tensor_scalar(et[:], et[:], 1.0, None, ALU.add).then_inc(one_c, 1)
            dve.wait_ge(one_c, 1)
            nc.vector.reciprocal(et[:], et[:]).then_inc(rec_c, 1)
            dve.wait_ge(rec_c, 1)
            nc.vector.tensor_tensor(sc[:], ct[:], et[:], ALU.mult).then_inc(silu_c, 1)
            dve.wait_ge(silu_c, 1)
            nc.vector.tensor_copy(scb[:], sc[:].unsqueeze(2).to_broadcast([P, NB, P])).then_inc(wide_c, 1)
            dve.wait_ge(modcol_mm, 1)
            nc.vector.tensor_copy(modcol[:, 0, :], psum[:, MISC, 0:NB]).then_inc(modcol_ready, 1)
            nc.vector.tensor_scalar(modcol[:, 1, :], psum[:, MISC, NB:2 * NB], 1.0, None, ALU.add
                                    ).then_inc(modcol_ready, 1)

            def first_stats(b):
                for t in range(BT):
                    ins = nc.vector.bn_stats(stats[:, t, :], xs[:, bass.ds(b * BT + t, 1), :])
                ins.then_inc(ln_stats, 1)
                dve.wait_ge(ln_stats, b + 1)
                dve.sem_inc(dve_waited, 1)
                for t in range(BT):
                    ins = nc.vector.bn_aggr(mv[:, t, :], stats[:, t, :])
                ins.then_inc(ln_aggr, 1)
                dve.wait_ge(ln_aggr, b + 1)
                nc.vector.tensor_scalar(vpe[:], mv[:, :, 1], EPS_LN, None, ALU.add).then_inc(ln_eps, 1)

            def normalise(b, half):
                c = b * 2 + half
                after(dve, xT_mm, c - 1)
                if half == 0:
                    dve.wait_ge(ln_rstd, b + 1)
                for i in range(4):
                    k = 4 * half + i
                    ins = nc.vector.tensor_scalar(xn[half][:, i, :], xs[:, bass.ds(c * 4 + i, 1), :],
                                                  mv[:, k:k + 1, 0], rstd[:, k:k + 1], ALU.subtract, ALU.mult)
                ins.then_inc(ln_norm, 1)

            def residues(b, half):
                c = b * 2 + half
                for j in range(2):
                    after(dve, part_lo, c * 2 + j - 3)
                    dve.wait_ge(part_hi, c * 2 + j + 1)
                    nc.vector.scalar_tensor_tensor(out=pres[half][j], in0=psum[:, 2 + 2 * j + half, :],
                                                   scalar=bqkv_s[:, j:j + 1], in1=parts[b % 2][half][j][:, 0, :],
                                                   op0=ALU.add, op1=ALU.subtract).then_inc(part_res, 1)
                dve.wait_ge(v_mm, c + 1)
                nc.vector.tensor_tensor(
                    vals[:, bass.ds(b * NG, NG), 4 * half:4 * half + 4, :].rearrange("p g t d -> p t g d"),
                    psum[:, 6 + half, :].rearrange("p (t g d) -> p t g d", t=4, g=NG),
                    bv_row[:].rearrange("p (a g d) -> p a g d", a=1, g=NG).to_broadcast([P, 4, NG, 32]),
                    ALU.add).then_inc(v_ready, 1)

            dve.wait_ge(x_in[0], 16)
            first_stats(0)
            normalise(0, 0)
            normalise(0, 1)
            dve.wait_ge(x_in[1], 16)
            first_stats(1)
            g = modrow[:, :, 0:4:3, :]
            dve.wait_ge(modrow_copied, 2 * NB)
            nc.vector.tensor_scalar(modrow[:, :, 2, :], modrow[:, :, 2, :], 1.0, None, ALU.add).then_inc(gates_ready, 1)
            nc.vector.tensor_scalar(gneg[:], g, -1.0, 0.25, ALU.mult, ALU.max).then_inc(gates_ready, 1)
            nc.vector.tensor_scalar(gsgn[:], g, 0.0, 2.0, ALU.is_ge, ALU.mult).then_inc(gates_ready, 1)
            dve.wait_ge(gates_ready, 3)
            nc.vector.tensor_tensor(gneg[:], gneg[:], g, ALU.max).then_inc(gates_ready, 1)
            dve.wait_ge(gates_ready, 4)
            for a in range(2):
                nc.vector.scalar_tensor_tensor(out=modrow[:, :, 3 * a, :], in0=gsgn[:, :, a, :], scalar=-1.0,
                                               in1=gneg[:, :, a, :], op0=ALU.add, op1=ALU.mult
                                               ).then_inc(gates_ready, 1)
            dve.wait_ge(w_in, 96)
            for q in range(1, 4):
                dve.wait_ge(x_in[q], 16)
            for b in range(NB - 2):
                for half in range(2):
                    normalise(b + 1, half)
                    residues(b, half)
                first_stats(b + 2)
            for half in range(2):
                normalise(NB - 1, half)
                residues(NB - 2, half)
            for half in range(2):
                residues(NB - 1, half)

            def maximum(n, u):
                dve.wait_ge(q_scores, n * NQU + u + 1)
                hp, kind = divmod(u, len(QUNITS))
                for i, k0, w, col, part in QUNITS[kind]:
                    ins = nc.vector.tensor_reduce(mx[:, part, 2 * hp:2 * hp + 2, i],
                                                  psum[:, QB[u % 2]:QB[u % 2] + 2, col:col + w], AX.X, ALU.max)
                ins.then_inc(maxed, 1)

            def negated_parts(n, first):
                k = n * 5
                dve.wait_ge(maxed, (n + 1) * NQU)
                if not first:
                    dve.wait_ge(mT_mm, n)
                nc.vector.tensor_tensor(mx[:, 0, :, 4:8], mx[:, 0, :, 4:8], mx[:, 1, :, 4:8], ALU.max
                                        ).then_inc(m_step, 1)
                dve.wait_ge(m_step, k + 1)
                nc.vector.tensor_scalar(mparts[:, 0, :, :], mx[:, 0, :, :], -1.0, None, ALU.mult).then_inc(m_step, 1)
                dve.wait_ge(m_step, k + 2)
                nc.vector.scalar_tensor_tensor(out=mres[:], in0=mx[:, 0, :, :], scalar=-1.0, in1=mparts[:, 0, :, :],
                                               op0=ALU.mult, op1=ALU.subtract).then_inc(m_step, 1)
                dve.wait_ge(m_step, k + 3)
                nc.vector.tensor_copy(mparts[:, 1, :, :], mres[:]).then_inc(m_step, 1)
                dve.wait_ge(m_step, k + 4)
                nc.vector.tensor_tensor(mparts[:, 2, :, :], mres[:], mparts[:, 1, :, :], ALU.subtract
                                        ).then_inc(m_step, 1)

            def normed(count, n, chunk):
                dve.wait_ge(oT_mm, count)
                o = psum[:, MISC, :].rearrange("p (t h d) -> p t h d", t=4, h=GH)
                nc.vector.reciprocal(rec[:].unsqueeze(3), o[:, :, :, HD:HD + 1]).then_inc(o_rec, 1)
                dve.wait_ge(o_rec, count)
                nc.vector.tensor_tensor(
                    ys[:, bass.ds(n, 1), 4 * chunk:4 * chunk + 4, :].rearrange("p n t (h d) -> p (n t) h d", h=GH),
                    o[:, :, :, 0:HD], rec[:].unsqueeze(3).to_broadcast([P, 4, GH, HD]),
                    ALU.mult).then_inc(o_norm, 1)

            rev_b = rev[:, 0:1, :].to_broadcast([P, BT, NE])

            def add_attention(b, half, bank):
                c = b * 2 + half
                dve.wait_ge(bias_in, c + 1)
                dve.wait_ge(proj_mm, c + 1)
                xv = xs[:, bass.ds(c * 4, 4), :]
                nc.vector.tensor_tensor(xv, psum[:, bank, :].rearrange("p (t d) -> p t d", t=4), xv,
                                        ALU.add).then_inc(x1_ready, 1)

            def second_stats(b, half):
                c = b * 2 + half
                dve.wait_ge(x1_ready, c + 1)
                dve.sem_inc(dve_waited, 1)
                for i in range(4):
                    ins = nc.vector.bn_stats(stats2[half][:, i, :], xs[:, bass.ds(c * 4 + i, 1), :])
                ins.then_inc(n2_stats, 1)

            def second_aggregates(b, half):
                c = b * 2 + half
                dve.wait_ge(n2_stats, c + 1)
                dve.sem_inc(dve_waited, 1)
                for i in range(4):
                    ins = nc.vector.bn_aggr(mv2[half][:, i, :], stats2[half][:, i, :])
                ins.then_inc(n2_aggr, 1)
                dve.wait_ge(n2_aggr, c + 1)
                nc.vector.tensor_scalar(vpe2[half][:], mv2[half][:, :, 1], EPS_LN, None, ALU.add
                                        ).then_inc(n2_step, 1)

            STEPS = 26
            steps = [0]

            def then(b, ins):
                steps[0] += 1
                ins.then_inc(route_step, 1)
                dve.wait_ge(route_step, b * STEPS + steps[0])

            def te(v, t=BT):
                return v.unsqueeze(2).to_broadcast([P, t, NE])

            def perm(v):
                return v.rearrange("p e t -> p t e")

            def shifted_logits(b, bank):
                steps[0] = 0
                dve.wait_ge(logit_mm, b + 1)
                nc.vector.tensor_copy(lg[:], psum[:, bank, 0:BT * NE].rearrange("p (t e) -> p t e", t=BT)
                                      ).then_inc(logit_ready, 1)
                dve.wait_ge(logit_ready, b + 1)
                then(b, nc.vector.tensor_reduce(m1b, lg[:], AX.X, ALU.max))
                nc.vector.tensor_tensor(lg[:], lg[:], te(m1b), ALU.subtract).then_inc(lg_shifted, 1)

            def first_choice(b):
                dve.wait_ge(exp_l, b + 1)
                then(b, nc.vector.tensor_reduce(smb, lg[:], AX.X, ALU.add))
                then(b, nc.vector.reciprocal(smb, smb))
                then(b, nc.vector.tensor_tensor(pr[:], lg[:], te(smb), ALU.mult))
                pm = pm1[:, bass.ds(b * BT, BT)]
                then(b, nc.vector.tensor_reduce(pm, pr[:], AX.X, ALU.max))
                then(b, nc.vector.tensor_tensor(eqb[:], pr[:], te(pm), ALU.is_equal))
                then(b, nc.vector.tensor_tensor(tvb[:], eqb[:], rev_b, ALU.mult))
                then(b, nc.vector.tensor_reduce(first1b, tvb[:], AX.X, ALU.max))
                then(b, nc.vector.tensor_tensor(oh1[:, bass.ds(b * BT, BT), :], rev_b, te(first1b), ALU.is_equal))

            def second_choice(b):
                pm = pm2[:, bass.ds(b * BT, BT)]
                one, two = (v[:, bass.ds(b * BT, BT), :] for v in (oh1, oh2))
                then(b, nc.vector.scalar_tensor_tensor(out=pr[:], in0=one, scalar=-2.0, in1=pr[:], op0=ALU.mult,
                                                       op1=ALU.add))
                then(b, nc.vector.tensor_reduce(pm, pr[:], AX.X, ALU.max))
                then(b, nc.vector.tensor_tensor(eqb[:], pr[:], te(pm), ALU.is_equal))
                then(b, nc.vector.tensor_tensor(tvb[:], eqb[:], rev_b, ALU.mult))
                then(b, nc.vector.tensor_reduce(first2b, tvb[:], AX.X, ALU.max))
                then(b, nc.vector.tensor_tensor(two, rev_b, te(first2b), ALU.is_equal))
                nc.vector.tensor_tensor(perm(maskbb[:]), one, two, ALU.add).then_inc(chosen, 1)

            def ranks(b, bank):
                dve.wait_ge(prefix_mm, b + 1)
                flat = [v[:].rearrange("p e t -> p (e t)") for v in (scanb, exclb, rankb)]
                tot = psum[:, bank, 64:128]
                then(b, nc.vector.tensor_tensor_scan(flat[0], onesf[:, 0:64], tot, 0.0, ALU.mult, ALU.add))
                then(b, nc.vector.tensor_tensor(flat[1], flat[0], tot, ALU.subtract))
                nc.vector.tensor_tensor(flat[2], psum[:, bank, 0:64], flat[1], ALU.add).then_inc(prefix_read, 1)
                then(b, nc.vector.tensor_tensor(shift[:], used[:], exclb[:, :, 0], ALU.subtract))
                dve.wait_ge(prefix_read, b + 1)
                then(b, nc.vector.tensor_tensor(rankb[:], rankb[:],
                                                shift[:].unsqueeze(2).to_broadcast([P, NE, BT]), ALU.add))
                nc.vector.tensor_tensor(used[:], shift[:], scanb[:, :, BT - 1], ALU.add)

            def slots(b):
                then(b, nc.vector.tensor_scalar(overb[:], rankb[:], float(CAP), FAR, ALU.is_ge, ALU.mult))
                then(b, nc.vector.tensor_tensor(overb[:], overb[:], rankb[:], ALU.add))
                then(b, nc.vector.tensor_tensor(overb[:], overb[:],
                                                rev[:, 1, :].unsqueeze(2).to_broadcast([P, NE, BT]), ALU.add))
                for k, (oh, tmp, sl) in enumerate(((oh1, eqb, first1b), (oh2, tvb, first2b))):
                    then(b, nc.vector.tensor_tensor(tmp[:], oh[:, bass.ds(b * BT, BT), :], perm(overb[:]), ALU.mult))
                    then(b, nc.vector.tensor_reduce(sl, tmp[:], AX.X, ALU.add))
                    nc.vector.tensor_copy(idxb[:, k, :], sl).then_inc(idx_ready, 1)
                assert steps[0] == STEPS

            def group(b, m, first, more, mix):
                n = b * NG + m
                p = b - 1
                for s in range(NKU):
                    for u in range(NQU):
                        if QSTEP[u] == s and more > 0:
                            maximum(n + 1, u)
                        if QSTEP[u] == s - NKU and more > 1:
                            maximum(n + 2, u)
                    if s == NSTEP and more > 0:
                        negated_parts(n + 1, False)
                    if mix and m == 3 and s == 6:
                        ranks(p, MISC)
                    if s == 11 and not first:
                        normed(n * 2, n - 1, 1)
                    if s == 24:
                        normed(n * 2 + 1, n, 0)
                    if mix and m == 1 and s in (4, 16):
                        add_attention(p, s // 16, MISC)
                    if mix and m == 1 and s in (6, 18):
                        second_stats(p, s // 18)
                    if mix and m == 1 and s in (8, 20):
                        second_aggregates(p, s // 20)
                    if mix and m == 2 and s == 16:
                        shifted_logits(p, MISC)
                    if mix and m == 2 and s == 24:
                        first_choice(p)
                    if mix and m == 3 and s == 2:
                        second_choice(p)
                    if mix and m == 3 and s == 8:
                        slots(p)

            for u in range(NQU):
                maximum(0, u)
            negated_parts(0, True)
            dve.wait_ge(iotas, 5)
            for i in range(2):
                nc.vector.tensor_copy(rev[:, i, :], rev_i[:, i, :]).then_inc(rev_ready, 1)
            dve.wait_ge(rev_ready, 2)
            for u in range(EARLY):
                maximum(1, u)
            for m in range(NG):
                group(0, m, m == 0, 2, False)
            with dve.Fori(1, NB - 1) as b:
                for m in range(NG):
                    group(b, m, False, 2, True)
            for m in range(NG):
                group(NB - 1, m, False, min(2, NG - 1 - m), True)
            normed(NN * 2, NN - 1, 1)

            b = NB - 1
            for half in range(2):
                add_attention(b, half, 2 + half)
            for half in range(2):
                second_stats(b, half)
                second_aggregates(b, half)
            for half in range(2):
                c = b * 2 + half
                h = rows[:, 0, 4 * half:4 * half + 4, 0:D]
                dve.wait_ge(rstd2_ready, c + 1)
                for i in range(4):
                    ins = nc.vector.tensor_scalar(h[:, i, :], xs[:, c * 4 + i, :], mv2[half][:, i, 0:1],
                                                  rstd2[half][:, i:i + 1], ALU.subtract, ALU.mult)
                ins.then_inc(last_norm, 1)
                dve.wait_ge(last_norm, 2 * half + 1)
                nc.vector.tensor_tensor(h, h, modrow[:, b:b + 1, 2, :].to_broadcast([P, 4, D]), ALU.mult
                                        ).then_inc(last_norm, 1)
                dve.wait_ge(last_norm, 2 * half + 2)
                nc.vector.tensor_tensor(h, h, modrow[:, b:b + 1, 1, :].to_broadcast([P, 4, D]), ALU.add
                                        ).then_inc(h2_ready, 1)
            shifted_logits(b, PV)
            first_choice(b)
            second_choice(b)
            ranks(b, MISC)
            dve.wait_ge(prefix_mm, NB)
            slots(b)

            last_steps = [0]

            def finish(ins):
                last_steps[0] += 1
                ins.then_inc(last_step, 1)
                dve.wait_ge(last_step, last_steps[0])

            finish(nc.vector.tensor_scalar(acc[:], used[:], float(CAP), None, ALU.is_gt))
            nc.vector.tensor_reduce(redo[:], acc[:], AX.X, ALU.max).then_inc(redo_ready, 1)
            finish(nc.vector.tensor_tensor(sm, pm1, pm2, ALU.add))
            finish(nc.vector.tensor_scalar(sm, sm, EPS, None, ALU.max))
            finish(nc.vector.reciprocal(sm, sm))
            nc.vector.tensor_tensor(w1s, pm1, sm, ALU.mult)
            finish(nc.vector.tensor_tensor(w2s, pm2, sm, ALU.mult))

            redo_steps = [0]

            def again_then(ins):
                redo_steps[0] += 1
                ins.then_inc(redo_step, 1)
                dve.wait_ge(redo_step, redo_steps[0])

            def counted(src, threshold, op):
                nc.vector.tensor_tensor(cmp_, src, threshold.unsqueeze(2).to_broadcast([P, NE, NT]), op
                                        ).then_inc(bis_step, 1)

            def prefix(k):
                dve.wait_ge(redo_prefix_mm, k + 1)
                tot = psum[:, 1 + k, 256:512]
                flat = [v.rearrange("p e t -> p (e t)") for v in (scan1, excl, rank)]
                again_then(nc.vector.tensor_tensor_scan(flat[0], onesf[:], tot, 0.0, ALU.mult, ALU.add))
                again_then(nc.vector.tensor_tensor(flat[1], tot, flat[0], ALU.subtract))
                again_then(nc.vector.tensor_tensor(rank, excl[:, :, 0:1].to_broadcast([P, NE, NT]), excl, ALU.subtract))
                again_then(nc.vector.tensor_tensor(flat[2], psum[:, 1 + k, 0:256], flat[2], ALU.add))

            dve.wait_ge(redo_ready, 1)
            again = dve.value_load(redo[0:1, 0:1], min_val=0, max_val=1)
            with dve.If(again > 0):
                nc.vector.tensor_tensor(wa, oh1[:], te(w1s, NT), ALU.mult)
                again_then(nc.vector.tensor_tensor(wb, oh2[:], te(w2s, NT), ALU.mult))
                nc.vector.scalar_tensor_tensor(out=eq, in0=oh1[:], scalar=-1.0, in1=oh2[:], op0=ALU.add, op1=ALU.add)
                again_then(nc.vector.tensor_tensor(wa, wa, wb, ALU.add))
                again_then(nc.vector.tensor_tensor(perm(wsel), wa, eq, ALU.add))
                nc.vector.memset(thr[:], 0)
                again_then(nc.vector.memset(bit[:], 1 << 29))
                with dve.Fori(0, 30) as i:
                    k = i * 6
                    nc.vector.tensor_tensor(cand[:], thr[:], bit[:], ALU.bitwise_or).then_inc(bis_step, 1)
                    dve.wait_ge(bis_step, k + 1)
                    counted(wsel, cand[:].bitcast(F32), ALU.is_ge)
                    dve.wait_ge(bis_step, k + 2)
                    nc.vector.tensor_reduce(acc[:], cmp_, AX.X, ALU.add).then_inc(bis_step, 1)
                    dve.wait_ge(bis_step, k + 3)
                    nc.vector.tensor_copy(part8[:], acc[:]).then_inc(bis_part, 1)
                    nc.vector.tensor_single_scalar(bit[:], bit[:], 1, ALU.logical_shift_right).then_inc(bis_step, 1)
                    dve.wait_ge(bis_count, i + 1)
                    nc.vector.scalar_tensor_tensor(out=acc[:], in0=psum[:, 0, 0:NE], scalar=float(CAP),
                                                   in1=cand[:].bitcast(F32), op0=ALU.is_ge, op1=ALU.mult
                                                   ).then_inc(bis_step, 1)
                    dve.wait_ge(bis_step, k + 5)
                    nc.vector.tensor_tensor(thr[:].bitcast(F32), thr[:].bitcast(F32), acc[:], ALU.max
                                            ).then_inc(bis_step, 1)
                    dve.wait_ge(bis_step, k + 6)
                thr_b = thr[:].bitcast(F32).unsqueeze(2).to_broadcast([P, NE, NT])
                again_then(nc.vector.tensor_tensor(keep, wsel, thr_b, ALU.is_gt))
                again_then(nc.vector.tensor_reduce(acc[:], keep, AX.X, ALU.add))
                nc.vector.tensor_copy(part8[:], acc[:]).then_inc(above_part, 1)
                again_then(nc.vector.tensor_tensor(cmp_, wsel, thr_b, ALU.is_equal))
                nc.vector.tensor_copy(maskb[:], cmp_).then_inc(redo_prefix_in, 1)
                dve.wait_ge(above_mm, 1)
                again_then(nc.vector.tensor_scalar(need[:], psum[:, 3, 0:NE], -1.0, float(CAP), ALU.mult, ALU.add))
                prefix(0)
                again_then(nc.vector.tensor_tensor(rank, rank, need[:].unsqueeze(2).to_broadcast([P, NE, NT]),
                                                   ALU.is_lt))
                again_then(nc.vector.tensor_tensor(rank, rank, cmp_, ALU.mult))
                again_then(nc.vector.tensor_tensor(keep, keep, rank, ALU.add))
                nc.vector.tensor_copy(maskb[:], keep).then_inc(redo_prefix_in, 1)
                prefix(1)
                again_then(nc.vector.tensor_tensor(rank, rank, rev[:, 1, :].unsqueeze(2).to_broadcast([P, NE, NT]),
                                                   ALU.add))
                again_then(nc.vector.tensor_scalar(rank, rank, -FAR, None, ALU.add))
                again_then(nc.vector.tensor_tensor(rank, rank, keep, ALU.mult))
                again_then(nc.vector.tensor_scalar(slot, rank, FAR, None, ALU.add))
                for k, (oh, sl, kp) in enumerate(((oh1[:], slot1, keep1), (oh2[:], slot2, keep2))):
                    again_then(nc.vector.tensor_tensor(prod, oh, perm(slot), ALU.mult))
                    again_then(nc.vector.tensor_reduce(sl, prod, AX.X, ALU.add))
                    nc.vector.tensor_copy(idx[:, k, :], sl).then_inc(redo_idx, 1)
                    again_then(nc.vector.tensor_tensor(wa, oh, perm(keep), ALU.mult))
                    again_then(nc.vector.tensor_reduce(kp, wa, AX.X, ALU.add))
            nc.vector.tensor_tensor(kw1, w1s, keep1, ALU.mult)
            finish(nc.vector.tensor_tensor(kw2, w2s, keep2, ALU.mult))
            finish(nc.vector.tensor_tensor(sm, kw1, kw2, ALU.add))
            finish(nc.vector.tensor_scalar(sm, sm, EPS, None, ALU.max))
            finish(nc.vector.reciprocal(sm, sm))
            nc.vector.tensor_tensor(kw1, kw1, sm, ALU.mult)
            finish(nc.vector.tensor_tensor(kw2, kw2, sm, ALU.mult))

            def low_rows(e, q, n):
                s0, ns = CH[n]
                cols = slice(s0 * P, (s0 + ns) * P)
                dve.wait_ge(x_high, e * 3 + n + 1)
                nc.vector.tensor_tensor(x_l[q][:, cols], psum[:, n % 2, 0:ns * P], x_h[q][:, cols].bitcast(F32),
                                        ALU.subtract).then_inc(x_low, 1)

            def keep_dests(e, q, j):
                dve.wait_ge(rows_in[q], j * 16 + 16)
                after(dve, sent[q], j * (16 * ST))
                nc.vector.tensor_copy(dest_of[q][:].unsqueeze(2), xr[q][:, :, D:ROW].bitcast(I32)
                                      ).then_inc(dest_kept, 1)

            def hidden(e, n, par):
                ns = CH[n][1]
                after(dve, down_mm, e * 3 + n - 1)
                for f in range(FC):
                    dve.wait_ge(silu_ready, (e * 3 + n) * FC + f + 1)
                    dve.wait_ge(up_mm, (e * 3 + n) * FC + f + 1)
                    nc.vector.tensor_tensor(hid[par][:, f, 0:ns * P], psum[:, 2 + 2 * (f % 2), 0:ns * P],
                                            sg[f % 2][:, 0:ns * P], ALU.mult).then_inc(hid_ready, 1)

            def expert(j, q, last):
                e = j * 2 + q
                hidden(e, 0, q)
                hidden(e, 1, 1 - q)
                hidden(e, 2, q)
                if not last:
                    low_rows(e + 1, 1 - q, 0)
                    low_rows(e + 1, 1 - q, 1)
                    low_rows(e + 1, 1 - q, 2)
                    keep_dests(e + 1, 1 - q, j + q)

            for n in range(3):
                low_rows(0, 0, n)
            keep_dests(0, 0, 0)
            for q in range(2):
                expert(0, q, False)
            with dve.Fori(1, NE // 2 - 1) as j:
                for q in range(2):
                    expert(j, q, False)
            for q in range(2):
                expert(NE // 2 - 1, q, q == 1)

            for b in range(NB):
                for t in range(b * BT, b * BT + BT):
                    dve.wait_ge(scaled, t + 1)
                    ins = nc.vector.scalar_tensor_tensor(out=g1[:, t, :], in0=g2[:, t, :], scalar=kw2[:, t:t + 1],
                                                         in1=g1[:, t, :], op0=ALU.mult, op1=ALU.add)
                ins.then_inc(summed, 1)
                dve.wait_ge(summed, b + 1)
                v = g1[:, b * BT:b * BT + BT, :]
                nc.vector.tensor_tensor(v, v, modrow[:, b:b + 1, 3, :].to_broadcast([P, BT, D]), ALU.mult
                                        ).then_inc(gated, 1)


def kernel(L0_attn_x, L0_attn_w_qkv, L0_attn_b_qkv, L0_attn_w_out, L0_attn_b_out, L0_ffn_router_weight,
           L0_ffn_ff_pre_act_weight, L0_ffn_gate_weight, L0_ffn_ff_post_act_weight, L0_c, L0_wmod):
    import numpy as np
    import concourse.bacc as bacc
    from concourse.bass_utils import run_bass_kernel_spmd

    order = np.arange(D).reshape(NG, GH, HD).transpose(0, 2, 1).reshape(-1)
    w, bq = np.asarray(L0_attn_w_qkv), np.asarray(L0_attn_b_qkv)
    rows = np.concatenate([order, D + order, np.arange(2 * D, 3 * D)])

    def turned(a):
        return np.ascontiguousarray(np.swapaxes(np.asarray(a), -1, -2))

    arrays = {
        "x": np.ascontiguousarray(L0_attn_x),
        "wqkvT": turned(w[rows]),
        "bqkv": np.ascontiguousarray(bq[rows].reshape(3, D).T),
        "bv": np.ascontiguousarray(bq[2 * D:].reshape(1, D)),
        "woT": turned(L0_attn_w_out),
        "bout": np.ascontiguousarray(L0_attn_b_out).reshape(1, D),
        "rT": turned(L0_ffn_router_weight),
        "w1T": turned(L0_ffn_ff_pre_act_weight),
        "wgT": turned(L0_ffn_gate_weight),
        "w2T": turned(L0_ffn_ff_post_act_weight),
        "cT": turned(L0_c),
        "wmod": np.ascontiguousarray(L0_wmod),
    }
    nc = bacc.Bacc("TRN2", target_bir_lowering=False, num_devices=1)
    args = {n: nc.dram_tensor(n, a.shape, mybir.dt.from_np(a.dtype), kind="ExternalInput").ap()
            for n, a in arrays.items()}
    args["out"] = nc.dram_tensor("out", [NB, S, D], F32, kind="ExternalOutput").ap()
    build(nc, **args)
    return run_bass_kernel_spmd(nc, [arrays], core_ids=[0]).results[0]["out"]
```
